# Optimizing a Trainium2 kernel written in Bass

```python
import numpy as np
import jax
import jax.numpy as jnp

def _softmax(x, axis=-1):
    return jax.nn.softmax(x, axis=axis)

def _gelu(x):
    return jax.nn.gelu(x, approximate=True)

def _silu(x):
    return jax.nn.silu(x)

def _sigmoid(x):
    return jax.nn.sigmoid(x)

def _layernorm(x, axis=-1, eps=1e-05):
    m = jnp.mean(x, axis=axis, keepdims=True)
    v = jnp.var(x, axis=axis, keepdims=True)
    return (x - m) / jnp.sqrt(v + eps)

def _scatter_add(tgt, idx, src, axis=0):
    return tgt.at[idx].add(src)

def _segment_sum(src, seg, n):
    return jax.ops.segment_sum(src, seg, n)
kernel_name = 'mk_lm_tower_d2_tok_ids256_r4_02d4af'

def setup_inputs(seed: int=0):
    np.random.seed(seed)
    _w = jnp.asarray

    def _rec_inputs():
        import jax
        import jax.numpy as jnp
        _rk = jax.random.key(seed)
        x = jax.random.randint(jax.random.fold_in(_rk, 1), (8, 512), 0, 7, jnp.int32)
        itok_BS_0_23 = jax.random.randint(jax.random.fold_in(_rk, 21), (8, 512), 0, 24, jnp.int32)
        itok_BS_0_11 = jax.random.randint(jax.random.fold_in(_rk, 22), (8, 512), 0, 12, jnp.int32)
        itok_BS_0_30 = jax.random.randint(jax.random.fold_in(_rk, 23), (8, 512), 0, 31, jnp.int32)
        return (x, itok_BS_0_23, itok_BS_0_11, itok_BS_0_30)
    x, itok_BS_0_23, itok_BS_0_11, itok_BS_0_30 = _rec_inputs()

    def _L0_tok_setup():
        import jax, jax.numpy as jnp
        import numpy as np
        import math
        B, S = (64, 512)
        HARM = 3
        N_PERIODS = 4
        FD = N_PERIODS * 2 * HARM
        TD = 64
        PERIODS = np.array([7.0, 24.0, 12.0, 1.0], dtype=np.float32)
        LN_EPS = 1e-05

        def _fourier_concat(dayofweek, hour, month, dayofmonth, hw, ph):
            t = jnp.stack([dayofweek, hour, month, dayofmonth]).astype(jnp.float32)
            periods = jnp.asarray(PERIODS)
            norm = 2.0 * math.pi * t / periods[:, None, None]
            h = jnp.arange(1, HARM + 1, dtype=jnp.float32)
            ang = norm[..., None] * h + ph[:, None, None, :]
            w = hw[:, None, None, :]
            f = jnp.stack([w * jnp.sin(ang), w * jnp.cos(ang)], axis=-1)
            return jnp.moveaxis(f, 0, 2).reshape(t.shape[1], t.shape[2], FD)
        key = jax.random.key(seed)
        ks = jax.random.split(key, 12)
        maxv = [7, 24, 12, 31]
        times = {n: jax.random.randint(ks[i], (B, S), 0, maxv[i], dtype=jnp.int32) for i, n in enumerate(['dayofweek', 'hour', 'month', 'dayofmonth'])}
        inp = dict(times)
        inp['hw'] = jax.random.uniform(ks[4], (N_PERIODS, HARM), dtype=jnp.float32) + 0.5
        inp['ph'] = jax.random.normal(ks[5], (N_PERIODS, HARM), dtype=jnp.float32) * 0.1
        inp['W1'] = jax.random.normal(ks[6], (FD, 2 * TD), dtype=jnp.float32) / math.sqrt(FD)
        inp['b1'] = jax.random.normal(ks[7], (2 * TD,), dtype=jnp.float32) * 0.01
        inp['W2'] = jax.random.normal(ks[8], (2 * TD, TD), dtype=jnp.float32) / math.sqrt(2 * TD)
        inp['b2'] = jax.random.normal(ks[9], (TD,), dtype=jnp.float32) * 0.01
        inp['gamma'] = jnp.ones((TD,), dtype=jnp.float32)
        inp['beta'] = jnp.zeros((TD,), dtype=jnp.float32)
        inp['Wres'] = jax.random.normal(ks[10], (FD, TD), dtype=jnp.float32) / math.sqrt(FD)
        inp['bres'] = jax.random.normal(ks[11], (TD,), dtype=jnp.float32) * 0.01
        return inp
    _L0_tok_all = _L0_tok_setup()
    _L0_tok_in = {k: v for k, v in _L0_tok_all.items() if k in ('hw', 'ph', 'W1', 'b1', 'W2', 'b2', 'gamma', 'beta', 'Wres', 'bres')}
    del _L0_tok_all

    def _L0_attn_setup():
        import jax, jax.numpy as jnp
        import numpy as np
        TEMPERATURE = 1.0
        W_BLEND = 0.8
        EPS = 1e-12

        def _l2norm(x):
            n = jnp.sqrt(jnp.sum(x * x, axis=-1, keepdims=True))
            return x / jnp.maximum(n, EPS)
        key = jax.random.key(seed)
        feats = jax.random.normal(key, (4, 512, 64), dtype=jnp.float32)
        return {'feats': feats}
    _L0_attn_all = _L0_attn_setup()
    _L0_attn_in = {k: v for k, v in _L0_attn_all.items() if k in ()}
    del _L0_attn_all

    def _L0_ffn_setup():
        import jax, jax.numpy as jnp
        import numpy as np
        DIM = 64
        HEADS = 8
        NUM_KEYS = 64
        NUM_KV = NUM_KEYS ** 2
        PK_TOPK = 16
        FINAL_TOPK = 16
        DIM_KEY = DIM // 2
        P = 2

        def _pk(x, Wq_pk, pk_keys):
            b, n, _ = x.shape
            q = (x @ Wq_pk).reshape(b, n, P, HEADS, DIM_KEY).transpose(2, 0, 1, 3, 4)
            sim = jnp.einsum('pbnhd,pkhd->pbnhk', q, pk_keys)
            scores, idx = jax.lax.top_k(sim, PK_TOPK)
            idx0 = idx[0]
            idx1 = idx[1] * NUM_KEYS
            index = (idx0[..., :, None] + idx1[..., None, :]).reshape(b, n, HEADS, PK_TOPK * PK_TOPK)
            score = (scores[0][..., :, None] + scores[1][..., None, :]).reshape(b, n, HEADS, PK_TOPK * PK_TOPK)
            final_scores, pk_idx = jax.lax.top_k(score, FINAL_TOPK)
            final_indices = jnp.take_along_axis(index, pk_idx, axis=-1)
            final_scores = jax.nn.softmax(final_scores, axis=-1)
            return (final_scores, final_indices)
        key = jax.random.key(seed)
        ks = jax.random.split(key, 7)
        b, n = (2, 256)
        std = 0.02
        x = jax.random.normal(ks[0], (b, n, DIM), dtype=jnp.float32)
        Wq_pk = jax.random.normal(ks[1], (DIM, P * HEADS * DIM_KEY), dtype=jnp.float32) * std
        pk_keys = jax.random.normal(ks[2], (P, NUM_KEYS, HEADS, DIM_KEY), dtype=jnp.float32) * std
        Wq = jax.random.normal(ks[3], (DIM, HEADS * DIM), dtype=jnp.float32) * std
        keys_table = jax.random.normal(ks[4], (NUM_KV * HEADS, DIM), dtype=jnp.float32) * std
        values_table = jax.random.normal(ks[5], (NUM_KV * HEADS, DIM), dtype=jnp.float32) * std
        Wo = jax.random.normal(ks[6], (DIM * HEADS, DIM), dtype=jnp.float32) * std
        return {'x': x, 'Wq_pk': Wq_pk, 'pk_keys': pk_keys, 'Wq': Wq, 'keys_table': keys_table, 'values_table': values_table, 'Wo': Wo}
    _L0_ffn_all = _L0_ffn_setup()
    _L0_ffn_in = {k: v for k, v in _L0_ffn_all.items() if k in ('Wq_pk', 'pk_keys', 'Wq', 'keys_table', 'values_table', 'Wo')}
    del _L0_ffn_all

    def _L1_attn_setup():
        import jax, jax.numpy as jnp
        import numpy as np
        DT_RANK = 16
        D_STATE = 16

        def silu(x):
            return x * jax.nn.sigmoid(x)

        def selective_scan(u, dt, A, Bm, C, D):
            Bsz, L, Di = u.shape
            N = A.shape[1]

            def step(h, xs):
                u_t, dt_t, B_t, C_t = xs
                dA = jnp.exp(dt_t[..., None] * A)
                h = h * dA + (dt_t * u_t)[..., None] * B_t[:, None, :]
                y = jnp.einsum('bdn,bn->bd', h, C_t)
                return (h, y)
            xs = (u.swapaxes(0, 1), dt.swapaxes(0, 1), Bm.swapaxes(0, 1), C.swapaxes(0, 1))
            h0 = jnp.zeros((Bsz, Di, N), dtype=u.dtype)
            _, ys = jax.lax.scan(step, h0, xs)
            return ys.swapaxes(0, 1) + u * D

        def ssm_branch(x, z, W_xp, W_dt, b_dt, A_log, D):
            xa = silu(x)
            xdbl = xa @ W_xp.T
            dt_low = xdbl[..., :DT_RANK]
            Bm = xdbl[..., DT_RANK:DT_RANK + D_STATE]
            C = xdbl[..., DT_RANK + D_STATE:]
            dt = jax.nn.softplus(dt_low @ W_dt.T + b_dt)
            A = -jnp.exp(A_log)
            y = selective_scan(xa, dt, A, Bm, C, D)
            return y * silu(z)
        key = jax.random.key(seed)
        ks = jax.random.split(key, 16)
        B, L, Dm, Di = (4, 1024, 64, 128)
        R, N = (DT_RANK, D_STATE)
        nrm = jax.random.normal
        inp = {'hidden_states': nrm(ks[0], (B, L, Dm), jnp.float32), 'W_in': nrm(ks[1], (4 * Di, Dm), jnp.float32) * 0.02, 'W_g': nrm(ks[2], (4 * Di, 4 * Di), jnp.float32) * 0.01, 'b_g': jnp.zeros((4 * Di,), jnp.float32), 'W_xp_f': nrm(ks[3], (R + 2 * N, Di), jnp.float32) * 0.02, 'W_xp_b': nrm(ks[4], (R + 2 * N, Di), jnp.float32) * 0.02, 'W_dt_f': nrm(ks[5], (Di, R), jnp.float32) * 0.25, 'b_dt_f': nrm(ks[6], (Di,), jnp.float32) * 0.1 - 4.0, 'W_dt_b': nrm(ks[7], (Di, R), jnp.float32) * 0.25, 'b_dt_b': nrm(ks[8], (Di,), jnp.float32) * 0.1 - 4.0, 'A_log_f': jnp.log(jnp.tile(jnp.arange(1, N + 1, dtype=jnp.float32), (Di, 1))), 'A_log_b': jnp.log(jnp.tile(jnp.arange(1, N + 1, dtype=jnp.float32), (Di, 1))), 'D_f': jnp.ones((Di,), jnp.float32), 'D_b': jnp.ones((Di,), jnp.float32), 'W_out': nrm(ks[9], (Dm, 2 * Di), jnp.float32) * 0.02}
        return inp
    _L1_attn_all = _L1_attn_setup()
    _L1_attn_in = {k: v for k, v in _L1_attn_all.items() if k in ('W_in', 'W_g', 'b_g', 'W_xp_f', 'W_xp_b', 'W_dt_f', 'b_dt_f', 'W_dt_b', 'b_dt_b', 'A_log_f', 'A_log_b', 'D_f', 'D_b', 'W_out')}
    del _L1_attn_all

    def _L1_ffn_setup():
        import jax, jax.numpy as jnp
        import numpy as np
        D_MODEL = 64
        EXPERT_DIM = 128
        NUM_EXPERTS = 8
        TOP_K = 2
        SEQ_LEN = 512
        BATCH = 2
        key = jax.random.key(seed)
        ks = jax.random.split(key, 8)
        s = 0.02
        x = jax.random.normal(ks[0], (SEQ_LEN, BATCH, D_MODEL), dtype=jnp.float32)
        Wg = jax.random.normal(ks[1], (D_MODEL, NUM_EXPERTS), dtype=jnp.float32) * s
        bg = jax.random.normal(ks[2], (NUM_EXPERTS,), dtype=jnp.float32) * s
        bias = jnp.zeros((NUM_EXPERTS,), dtype=jnp.float32)
        W1 = jax.random.normal(ks[3], (NUM_EXPERTS, D_MODEL, EXPERT_DIM), dtype=jnp.float32) * s
        b1 = jax.random.normal(ks[4], (NUM_EXPERTS, EXPERT_DIM), dtype=jnp.float32) * s
        W2 = jax.random.normal(ks[5], (NUM_EXPERTS, EXPERT_DIM, D_MODEL), dtype=jnp.float32) * s
        b2 = jax.random.normal(ks[6], (NUM_EXPERTS, D_MODEL), dtype=jnp.float32) * s
        return {'x': x, 'Wg': Wg, 'bg': bg, 'bias': bias, 'W1': W1, 'b1': b1, 'W2': W2, 'b2': b2}
    _L1_ffn_all = _L1_ffn_setup()
    _L1_ffn_in = {k: v for k, v in _L1_ffn_all.items() if k in ('Wg', 'bg', 'bias', 'W1', 'b1', 'W2', 'b2')}
    del _L1_ffn_all
    return {'x': x, 'itok_BS_0_23': itok_BS_0_23, 'itok_BS_0_11': itok_BS_0_11, 'itok_BS_0_30': itok_BS_0_30, 'L0_tok_hw': _L0_tok_in['hw'], 'L0_tok_ph': _L0_tok_in['ph'], 'L0_tok_W1': _L0_tok_in['W1'], 'L0_tok_b1': _L0_tok_in['b1'], 'L0_tok_W2': _L0_tok_in['W2'], 'L0_tok_b2': _L0_tok_in['b2'], 'L0_tok_gamma': _L0_tok_in['gamma'], 'L0_tok_beta': _L0_tok_in['beta'], 'L0_tok_Wres': _L0_tok_in['Wres'], 'L0_tok_bres': _L0_tok_in['bres'], 'L0_ffn_Wq_pk': _L0_ffn_in['Wq_pk'], 'L0_ffn_pk_keys': _L0_ffn_in['pk_keys'], 'L0_ffn_Wq': _L0_ffn_in['Wq'], 'L0_ffn_keys_table': _L0_ffn_in['keys_table'], 'L0_ffn_values_table': _L0_ffn_in['values_table'], 'L0_ffn_Wo': _L0_ffn_in['Wo'], 'L1_attn_W_in': _L1_attn_in['W_in'], 'L1_attn_W_g': _L1_attn_in['W_g'], 'L1_attn_b_g': _L1_attn_in['b_g'], 'L1_attn_W_xp_f': _L1_attn_in['W_xp_f'], 'L1_attn_W_xp_b': _L1_attn_in['W_xp_b'], 'L1_attn_W_dt_f': _L1_attn_in['W_dt_f'], 'L1_attn_b_dt_f': _L1_attn_in['b_dt_f'], 'L1_attn_W_dt_b': _L1_attn_in['W_dt_b'], 'L1_attn_b_dt_b': _L1_attn_in['b_dt_b'], 'L1_attn_A_log_f': _L1_attn_in['A_log_f'], 'L1_attn_A_log_b': _L1_attn_in['A_log_b'], 'L1_attn_D_f': _L1_attn_in['D_f'], 'L1_attn_D_b': _L1_attn_in['D_b'], 'L1_attn_W_out': _L1_attn_in['W_out'], 'L1_ffn_Wg': _L1_ffn_in['Wg'], 'L1_ffn_bg': _L1_ffn_in['bg'], 'L1_ffn_bias': _L1_ffn_in['bias'], 'L1_ffn_W1': _L1_ffn_in['W1'], 'L1_ffn_b1': _L1_ffn_in['b1'], 'L1_ffn_W2': _L1_ffn_in['W2'], 'L1_ffn_b2': _L1_ffn_in['b2']}

def reference(x, itok_BS_0_23, itok_BS_0_11, itok_BS_0_30, L0_tok_hw, L0_tok_ph, L0_tok_W1, L0_tok_b1, L0_tok_W2, L0_tok_b2, L0_tok_gamma, L0_tok_beta, L0_tok_Wres, L0_tok_bres, L0_ffn_Wq_pk, L0_ffn_pk_keys, L0_ffn_Wq, L0_ffn_keys_table, L0_ffn_values_table, L0_ffn_Wo, L1_attn_W_in, L1_attn_W_g, L1_attn_b_g, L1_attn_W_xp_f, L1_attn_W_xp_b, L1_attn_W_dt_f, L1_attn_b_dt_f, L1_attn_W_dt_b, L1_attn_b_dt_b, L1_attn_A_log_f, L1_attn_A_log_b, L1_attn_D_f, L1_attn_D_b, L1_attn_W_out, L1_ffn_Wg, L1_ffn_bg, L1_ffn_bias, L1_ffn_W1, L1_ffn_b1, L1_ffn_W2, L1_ffn_b2):
    import jax
    import jax.numpy as jnp

    def _L0_tok_ref(dayofweek, hour, month, dayofmonth, hw, ph, W1, b1, W2, b2, gamma, beta, Wres, bres):
        import jax, jax.numpy as jnp
        import numpy as np
        import math
        B, S = (64, 512)
        HARM = 3
        N_PERIODS = 4
        FD = N_PERIODS * 2 * HARM
        TD = 64
        PERIODS = np.array([7.0, 24.0, 12.0, 1.0], dtype=np.float32)
        LN_EPS = 1e-05

        def _fourier_concat(dayofweek, hour, month, dayofmonth, hw, ph):
            t = jnp.stack([dayofweek, hour, month, dayofmonth]).astype(jnp.float32)
            periods = jnp.asarray(PERIODS)
            norm = 2.0 * math.pi * t / periods[:, None, None]
            h = jnp.arange(1, HARM + 1, dtype=jnp.float32)
            ang = norm[..., None] * h + ph[:, None, None, :]
            w = hw[:, None, None, :]
            f = jnp.stack([w * jnp.sin(ang), w * jnp.cos(ang)], axis=-1)
            return jnp.moveaxis(f, 0, 2).reshape(t.shape[1], t.shape[2], FD)
        x = _fourier_concat(dayofweek, hour, month, dayofmonth, hw, ph)
        h1 = jax.nn.relu(jnp.einsum('bsf,fd->bsd', x, W1) + b1)
        h2 = jnp.einsum('bsd,dt->bst', h1, W2) + b2
        mu = jnp.mean(h2, axis=-1, keepdims=True)
        var = jnp.mean(jnp.square(h2 - mu), axis=-1, keepdims=True)
        ln = (h2 - mu) * jax.lax.rsqrt(var + LN_EPS) * gamma + beta
        residual = jnp.einsum('bsf,ft->bst', x, Wres) + bres
        return ln + 0.1 * residual

    def _L0_attn_ref(feats):
        import jax, jax.numpy as jnp
        import numpy as np
        TEMPERATURE = 1.0
        W_BLEND = 0.8
        EPS = 1e-12

        def _l2norm(x):
            n = jnp.sqrt(jnp.sum(x * x, axis=-1, keepdims=True))
            return x / jnp.maximum(n, EPS)
        B, N, C = feats.shape
        f = _l2norm(feats.reshape(B * N, C))
        scores = jnp.matmul(f, f.T) / TEMPERATURE
        attn = jax.nn.softmax(scores, axis=-1)
        feats_att = jnp.matmul(attn, f)
        feats_fcm = f * W_BLEND + feats_att * (1.0 - W_BLEND)
        return _l2norm(feats_fcm.reshape(B, N, C))

    def _L0_ffn_ref(x, Wq_pk, pk_keys, Wq, keys_table, values_table, Wo):
        import jax, jax.numpy as jnp
        import numpy as np
        DIM = 64
        HEADS = 8
        NUM_KEYS = 64
        NUM_KV = NUM_KEYS ** 2
        PK_TOPK = 16
        FINAL_TOPK = 16
        DIM_KEY = DIM // 2
        P = 2

        def _pk(x, Wq_pk, pk_keys):
            b, n, _ = x.shape
            q = (x @ Wq_pk).reshape(b, n, P, HEADS, DIM_KEY).transpose(2, 0, 1, 3, 4)
            sim = jnp.einsum('pbnhd,pkhd->pbnhk', q, pk_keys)
            scores, idx = jax.lax.top_k(sim, PK_TOPK)
            idx0 = idx[0]
            idx1 = idx[1] * NUM_KEYS
            index = (idx0[..., :, None] + idx1[..., None, :]).reshape(b, n, HEADS, PK_TOPK * PK_TOPK)
            score = (scores[0][..., :, None] + scores[1][..., None, :]).reshape(b, n, HEADS, PK_TOPK * PK_TOPK)
            final_scores, pk_idx = jax.lax.top_k(score, FINAL_TOPK)
            final_indices = jnp.take_along_axis(index, pk_idx, axis=-1)
            final_scores = jax.nn.softmax(final_scores, axis=-1)
            return (final_scores, final_indices)
        b, n, d = x.shape
        q = (x @ Wq).reshape(b, n, HEADS, DIM) * DIM ** (-0.5)
        kv_scores, indices = _pk(x, Wq_pk, pk_keys)
        offsets = jnp.arange(HEADS, dtype=indices.dtype) * NUM_KV
        ind = indices + offsets[None, None, :, None]
        k = jnp.einsum('bnhk,bnhkd->bnhd', kv_scores, keys_table[ind])
        v = jnp.einsum('bnhk,bnhkd->bnhd', kv_scores, values_table[ind])
        sim = jnp.einsum('bihd,bjhd->bhij', q, k)
        neg = -jnp.finfo(sim.dtype).max
        causal = jnp.tril(jnp.ones((n, n), dtype=bool))
        sim = jnp.where(causal, sim, neg)
        attn = jax.nn.softmax(sim, axis=-1)
        out = jnp.einsum('bhij,bjhd->bhid', attn, v)
        out = out.transpose(0, 2, 1, 3).reshape(b, n, HEADS * DIM)
        return out @ Wo

    def _L1_attn_ref(hidden_states, W_in, W_g, b_g, W_xp_f, W_xp_b, W_dt_f, b_dt_f, W_dt_b, b_dt_b, A_log_f, A_log_b, D_f, D_b, W_out):
        import jax, jax.numpy as jnp
        import numpy as np
        DT_RANK = 16
        D_STATE = 16

        def silu(x):
            return x * jax.nn.sigmoid(x)

        def selective_scan(u, dt, A, Bm, C, D):
            Bsz, L, Di = u.shape
            N = A.shape[1]

            def step(h, xs):
                u_t, dt_t, B_t, C_t = xs
                dA = jnp.exp(dt_t[..., None] * A)
                h = h * dA + (dt_t * u_t)[..., None] * B_t[:, None, :]
                y = jnp.einsum('bdn,bn->bd', h, C_t)
                return (h, y)
            xs = (u.swapaxes(0, 1), dt.swapaxes(0, 1), Bm.swapaxes(0, 1), C.swapaxes(0, 1))
            h0 = jnp.zeros((Bsz, Di, N), dtype=u.dtype)
            _, ys = jax.lax.scan(step, h0, xs)
            return ys.swapaxes(0, 1) + u * D

        def ssm_branch(x, z, W_xp, W_dt, b_dt, A_log, D):
            xa = silu(x)
            xdbl = xa @ W_xp.T
            dt_low = xdbl[..., :DT_RANK]
            Bm = xdbl[..., DT_RANK:DT_RANK + D_STATE]
            C = xdbl[..., DT_RANK + D_STATE:]
            dt = jax.nn.softplus(dt_low @ W_dt.T + b_dt)
            A = -jnp.exp(A_log)
            y = selective_scan(xa, dt, A, Bm, C, D)
            return y * silu(z)
        xz = hidden_states @ W_in.T
        xz = xz + (jnp.mean(xz, axis=1, keepdims=True) @ W_g.T + b_g)
        x_f, z_f, x_b, z_b = jnp.split(xz, 4, axis=-1)
        y_f = ssm_branch(x_f, z_f, W_xp_f, W_dt_f, b_dt_f, A_log_f, D_f)
        y_b = ssm_branch(x_b[:, ::-1], z_b[:, ::-1], W_xp_b, W_dt_b, b_dt_b, A_log_b, D_b)[:, ::-1]
        return jnp.concatenate([y_f, y_b], axis=-1) @ W_out.T

    def _L1_ffn_ref(x, Wg, bg, bias, W1, b1, W2, b2):
        import jax, jax.numpy as jnp
        import numpy as np
        D_MODEL = 64
        EXPERT_DIM = 128
        NUM_EXPERTS = 8
        TOP_K = 2
        SEQ_LEN = 512
        BATCH = 2
        x_flat = x.reshape(-1, D_MODEL)
        gate_logits = x_flat @ Wg + bg + bias
        topk_vals, topk_idx = jax.lax.top_k(gate_logits, TOP_K)
        topk_w = jax.nn.softmax(topk_vals, axis=-1)
        combine = (jax.nn.one_hot(topk_idx, NUM_EXPERTS, dtype=x.dtype) * topk_w[..., None]).sum(axis=1)
        h = jax.nn.relu(jnp.einsum('td,edh->teh', x_flat, W1) + b1)
        y = jnp.einsum('teh,ehd->ted', h, W2) + b2
        out = jnp.einsum('ted,te->td', y, combine)
        return out.reshape(x.shape)
    h = _L0_tok_ref(x, itok_BS_0_23, itok_BS_0_11, itok_BS_0_30, L0_tok_hw, L0_tok_ph, L0_tok_W1, L0_tok_b1, L0_tok_W2, L0_tok_b2, L0_tok_gamma, L0_tok_beta, L0_tok_Wres, L0_tok_bres)
    h = h + _L0_attn_ref(_layernorm(h, axis=-1))
    h = h + _L0_ffn_ref(_layernorm(h, axis=-1), L0_ffn_Wq_pk, L0_ffn_pk_keys, L0_ffn_Wq, L0_ffn_keys_table, L0_ffn_values_table, L0_ffn_Wo)
    h = h + _L1_attn_ref(_layernorm(h, axis=-1), L1_attn_W_in, L1_attn_W_g, L1_attn_b_g, L1_attn_W_xp_f, L1_attn_W_xp_b, L1_attn_W_dt_f, L1_attn_b_dt_f, L1_attn_W_dt_b, L1_attn_b_dt_b, L1_attn_A_log_f, L1_attn_A_log_b, L1_attn_D_f, L1_attn_D_b, L1_attn_W_out)
    h = h + _L1_ffn_ref(_layernorm(h, axis=-1), L1_ffn_Wg, L1_ffn_bg, L1_ffn_bias, L1_ffn_W1, L1_ffn_b1, L1_ffn_W2, L1_ffn_b2)
    return h

_drawn_inputs = setup_inputs


def setup_inputs(seed=0):
    import zlib

    import numpy as np

    out = dict(_drawn_inputs(seed))
    spreads = {'L0_tok_gamma': (1.0, 0.2),
     'L0_tok_beta': (0.0, 0.1),
     'L1_attn_b_g': (0.0, 0.8),
     'L1_attn_D_f': (1.0, 0.6),
     'L1_attn_D_b': (1.0, 0.6),
     'L1_ffn_bias': (0.0, 2.0)}
    factors = {'L0_tok_b1': 3.628,
     'L0_tok_bres': 8.0,
     'L0_ffn_Wq_pk': 8.0,
     'L0_ffn_pk_keys': 8.0,
     'L0_ffn_Wq': 64.0,
     'L0_ffn_keys_table': 64.0,
     'L0_ffn_values_table': 8.0,
     'L0_ffn_Wo': 8.0,
     'L1_attn_W_in': 8.0,
     'L1_attn_W_g': 8.0,
     'L1_attn_W_xp_f': 8.0,
     'L1_attn_W_xp_b': 8.0,
     'L1_attn_W_dt_f': 8.0,
     'L1_attn_b_dt_f': 8.0,
     'L1_attn_W_dt_b': 8.0,
     'L1_attn_b_dt_b': 8.0,
     'L1_attn_A_log_f': 8.0,
     'L1_attn_A_log_b': 8.0,
     'L1_attn_W_out': 8.0,
     'L1_ffn_Wg': 28.976,
     'L1_ffn_bg': 64.0,
     'L1_ffn_W1': 36.264,
     'L1_ffn_b1': 64.0,
     'L1_ffn_W2': 29.808,
     'L1_ffn_b2': 37.552}
    for name, (base, spread) in spreads.items():
        noise = np.random.default_rng([zlib.crc32(name.encode()), seed]).standard_normal(out[name].shape)
        drawn = base * np.exp(spread * noise) if base else spread * noise
        out[name] = jnp.asarray(drawn.astype(out[name].dtype))
    for name, factor in factors.items():
        out[name] = (out[name] * factor).astype(out[name].dtype)
    return out
```

```python
from contextlib import ExitStack

import concourse.bass as bass
from concourse import mybir

ALU = mybir.AluOpType
ACT = mybir.ActivationFunctionType
AX = mybir.AxisListType
F32 = mybir.dt.float32
BF16 = mybir.dt.bfloat16
I32 = mybir.dt.int32
U32 = mybir.dt.uint32

P = 128
D = 64
B, S = 8, 512
TILES = B * S // P
TPB = S // P
EPS = 1e-5

HARM, NPER = 3, 4
FD = NPER * 2 * HARM
GROUPS = 4
GTOK = B * S // GROUPS
TWO_PI = 6.283185307179586
ROUND = 12582912.0
PI_A, PI_B, PI_C = 6.28125, 0.0019350051879882812, 3.019916050561733e-07
PI_MAX = 3.1415925

HEADS = 8
NKEY = 64
TOPK = 16
KDIM = 32
ROWS = 2 * HEADS
CAND = [TOPK // (a + 1) for a in range(TOPK)]
NCAND = sum(CAND)
WIDE = sum(1 for n in CAND if n > 1)
LOW = -3.0e38
SLOTS = 4
RING = 8
XRING = 4
LOOKUP = 2

ROUTE_STEPS = 12
ROUTING_STEPS = 3 + TPB * ROUTE_STEPS
ATTEND_STEPS = HEADS + 5
GATES_STEPS, OUT_STEPS, EXPERTS_STEPS = 8, 2, 12

DI, NST, RANK = 128, 16, 16
DIRECTION_STEPS = NST + 6
TOWER_STEPS = TPB * ATTEND_STEPS + GATES_STEPS + 2 * DIRECTION_STEPS + OUT_STEPS + EXPERTS_STEPS
ATANH = (2.0, 0.6666632294654846, 0.4002459645271301, 0.27965158224105835, 0.28157779574394226)

EXP, EDIM = 8, 128


def program(nc, A, out):
    ctx = ExitStack()
    with ctx:
        def sb(name, shape, dt=F32):
            return ctx.enter_context(nc.sbuf_tensor(name, shape, dt))

        def sem(name):
            return ctx.enter_context(nc.semaphore(name))

        bank = [ctx.enter_context(nc.psum_tensor(f"bank{i}", [P, 512], F32)) for i in range(8)]

        h = sb("h", [P, TILES, D])
        xT = sb("xT", [D, XRING * S])
        idf = sb("idf", [P, P])
        idb = sb("idb", [P, P], BF16)
        causal = sb("causal", [P, P], BF16)
        cand_no = sb("cand_no", [P, NCAND])
        head_base = sb("head_base", [P, HEADS, TOPK])
        exp_no = sb("exp_no", [P, EXP])
        ones = sb("ones", [1, P])
        spread3 = sb("spread3", [P, 2 * NST], BF16)

        w_feat = sb("w_feat", [P, 2 * HARM])
        tW1 = sb("tW1", [P, 128])
        tWres = sb("tWres", [P, D])
        tW2 = sb("tW2", [128, D])
        tb1 = sb("tb1", [P, 1])
        trow = sb("trow", [P, 4, D])
        wqpk = sb("wqpk", [D, ROWS * KDIM])
        keys = sb("keys", [P, 4, 4 * NKEY])
        wq = sb("wq", [D, HEADS * D])
        wo = sb("wo", [P, 4, D])
        winT = sb("winT", [D, 4 * DI])
        wgT = sb("wgT", [P, 4, 4 * DI])
        bg_m = sb("bg_m", [P, 4])
        wxpT = sb("wxpT", [P, 2, P])
        wdtT = sb("wdtT", [RANK, 2, DI])
        bdt = sb("bdt", [P, 2])
        negA = sb("negA", [P, 2, NST])
        Dskip = sb("Dskip", [P, 2])
        woutT = sb("woutT", [P, 2, D])
        eWg = sb("eWg", [D, EXP])
        ebias = sb("ebias", [P, 2, EXP])
        eW1 = sb("eW1", [D, EXP, EDIM])
        eb1 = sb("eb1", [P, EXP])
        eW2 = sb("eW2", [P, EXP, D])
        eb2 = sb("eb2", [1, EXP * D])

        rows = sb("rows", [P, SLOTS, TOPK, 2 * D])
        ids_ring = sb("ids_ring", [P, RING, HEADS * TOPK], U32)
        ids_now = sb("ids_now", [P, 2, HEADS * TOPK], U32)
        w_ring = sb("w_ring", [P, RING, HEADS * TOPK])
        qpkT = sb("qpkT", [P, 4, P])
        sim = sb("sim", [P, ROWS, NKEY])
        best = sb("best", [P, ROWS, TOPK])
        besti = sb("besti", [P, ROWS, TOPK], U32)
        bestf = sb("bestf", [P, ROWS, TOPK])
        cval = sb("cval", [P, HEADS, NCAND])
        cid = sb("cid", [P, HEADS, NCAND])
        fval = sb("fval", [P, HEADS, TOPK])
        fpos = sb("fpos", [P, HEADS, TOPK], U32)
        fposf = sb("fposf", [P, HEADS, TOPK])
        look = sb("look", [P, LOOKUP * TOPK * NCAND])
        assert LOOKUP * TOPK * NCAND >= ROWS * NKEY
        sim2 = look[:, 0:ROWS * NKEY].rearrange("p (r k) -> p r k", r=ROWS)
        cval2 = look[:, 0:HEADS * NCAND].rearrange("p (r k) -> p r k", r=HEADS)
        shift = sb("shift", [P, HEADS, TOPK])
        fsum = sb("fsum", [P, HEADS])
        k_now = sb("k_now", [P, HEADS * D])
        kT = sb("kT", [P, 2, 4, S])
        val = sb("val", [P, 2, TPB, HEADS, D])

        prob = sb("prob", [P, 2, S])
        probT = sb("probT", [P, 2, 4, P])
        o_now = sb("o_now", [P, HEADS * D])
        oT = sb("oT", [P, 4, P])
        negmax = sb("negmax", [P, 2])
        psum_row = sb("psum_row", [P, 4])
        qz = sb("qz", [P, HEADS, P])
        rrow = sb("rrow", [P, 1])

        xz = sb("xz", [P, 4, S])
        gate = sb("gate", [P, 4, S])
        xsum = sb("xsum", [P, 4])
        xmean = sb("xmean", [P, 4])
        gsh = sb("gsh", [P, 4])
        ngsh = sb("ngsh", [P, 4])
        bc3 = sb("bc3", [P, S], BF16)
        dt = sb("dt", [P, S])
        dtu = sb("dtu", [P, S])
        mwork = sb("mwork", [P, 8, S])
        dA = mwork[:, 0:2, :]
        hC = mwork[:, 2:4, :]
        dBu = mwork[:, 4, :]
        hst = mwork[:, 5, :]
        bc_rest = mwork[:, 6, :]
        dt_low = mwork[0:RANK, 7, :]
        sp_relu, sp_u, sp_w, sp_l = (mwork[:, i, :] for i in (0, 1, 2, 3))
        hid = mwork

        def norm_set(tag):
            return dict(
                xc=sb(f"xc_{tag}", [P, TPB, D]), sq=sb(f"sq_{tag}", [P, TPB, D]),
                s=sb(f"s_{tag}", [P, TPB]), v=sb(f"v_{tag}", [P, TPB]), y0=sb(f"y0_{tag}", [P, TPB]),
                t=sb(f"t_{tag}", [P, TPB]), r=sb(f"r_{tag}", [P, TPB]), l=sb(f"l_{tag}", [P, TPB]))
        NR, NM = norm_set("r"), norm_set("m")
        xt4 = dtu[0:D, :]
        lg = sb("lg", [P, TPB, EXP])
        lmax = sb("lmax", [P, TPB, 8])
        lidx = sb("lidx", [P, TPB, 8], U32)
        lidf = sb("lidf", [P, TPB, 8])
        tw = sb("tw", [P, 4, TPB])
        comb = sb("comb", [P, 2, TPB, EXP])
        ymix = sb("ymix", [P, TPB, D])
        hout = sb("hout", [P, TPB, D])

        flat = rows[:, :, :, :].rearrange("p s k d -> p (s k d)")
        fT = flat[0:D, 0:B * S]
        f1 = flat[:, B * S:B * S + TILES * (D + 1)].rearrange("p (t d) -> p t d", d=D + 1)
        E0 = B * S + TILES * (D + 1)
        esc = flat[:, E0:E0 + 3 * 512].rearrange("p (n k) -> p n k", n=3)
        uT = mwork[0:D + 1, 7, :]
        feat = xz[:, 0:2, :].rearrange("p a s -> p (a s)")
        idsb = xz[:, 2:4, :].rearrange("p a s -> p (a s)").bitcast(I32)
        ang = gate[:, 0:2, :].rearrange("p a s -> p (a s)")
        turn = gate[:, 2:4, :].rearrange("p a s -> p (a s)")
        feat_now = mwork[:, 0, :]
        h1 = mwork[:, 1:3, :]

        loaded = sem("loaded")
        ids_zeroed = sem("ids_zeroed")
        ids_in = sem("ids_in")
        consts = sem("consts")
        weights_zeroed = sem("weights_zeroed")
        angle_done, feat_done, chunk_in = sem("angle_done"), sem("feat_done"), sem("chunk_in")
        h1_ps, h1_sb, h2_ps, h2_read = sem("h1_ps"), sem("h1_sb"), sem("h2_ps"), sem("h2_read")
        t_var, t_rstd = sem("t_var"), sem("t_rstd")
        u_var, u_rstd, u_sq, u_rl2 = sem("u_var"), sem("u_rstd"), sem("u_sq"), sem("u_rl2")
        f_done, f1_in, fT_ps, fT_sb = sem("f_done"), sem("f1_in"), sem("fT_ps"), sem("fT_sb")
        mixed = sem("mixed")
        score_ps, score_exp, mix_ps, mix_sb = sem("score_ps"), sem("score_exp"), sem("mix_ps"), sem("mix_sb")
        mixT_ps, mixT_read, m_sq, m_rl2 = sem("mixT_ps"), sem("mixT_read"), sem("m_sq"), sem("m_rl2")
        r_var, r_rstd, r_x, r_xT_ps, r_xT = (sem("r_" + x) for x in ("var", "rstd", "x", "xT_ps", "xT"))
        q_ps, q_sb, sim_ps, sim_sb = sem("q_ps"), sem("q_sb"), sem("sim_ps"), sem("sim_sb")
        picked, shifted, exped, ids_ready = sem("picked"), sem("shifted"), sem("exped"), sem("ids_ready")
        landed = [sem(f"landed{i}") for i in range(SLOTS)]
        weighted, summed, kv_sb, kT_ps, kT_sb = (sem(x) for x in ("weighted", "summed", "kv_sb", "kT_ps", "kT_sb"))
        aq_ps, aq_sb = sem("aq_ps"), sem("aq_sb")
        a_s, a_max, a_exp, a_T, a_Tsb, a_o, a_norm = (sem("a_" + x) for x in ("s", "max", "exp", "T", "Tsb", "o", "norm"))
        ao_T, ao_sb, ao_ps, ao_h = sem("ao_T"), sem("ao_sb"), sem("ao_ps"), sem("ao_h")
        m_var, m_rstd, m_x, m_xT_ps, m_xT = (sem("m_" + x) for x in ("var", "rstd", "x", "xT_ps", "xT"))
        xz_ps, xz_sb, mean_in, gsh_ps, gsh_in, sig_e, act_in = (
            sem(x) for x in ("xz_ps", "xz_sb", "mean_in", "gsh_ps", "gsh_in", "sig_e", "act_in"))
        xd_ps, xd_sb, dt_ps, sp_e, dt_in = (sem(x) for x in ("xd_ps", "xd_sb", "dt_ps", "sp_e", "dt_in"))
        bc_in = sem("bc_in")
        B_ps, C_ps, dA_in, dBu_in, scanned, hC_in, y_ps = (
            sem(x) for x in ("B_ps", "C_ps", "dA_in", "dBu_in", "scanned", "hC_in", "y_ps"))
        y_in, m_out_ps, m_done = sem("y_in"), sem("m_out_ps"), sem("m_done")
        e_var, e_rstd, e_x, e_xT_ps, e_xT = (sem("e_" + x) for x in ("var", "rstd", "x", "xT_ps", "xT"))
        lg_ps, lg_read, top_d, top_e, hid_ps, hid_sb, y2_ps, y2_read, e_done = (
            sem(x) for x in ("lg_ps", "lg_read", "top_d", "top_e", "hid_ps", "hid_sb", "y2_ps", "y2_read", "e_done"))
        stored = sem("stored")

        block = ctx.enter_context(nc.Block())

        def count(n):
            return max(n, 0) if isinstance(n, int) else n

        def idle(steps):
            for _ in range(steps):
                yield

        def schedule(eng, sums, route_norm, route, attend, gates, direction, mix_out, experts):
            turn_kT, weigh, add_up = sums

            def routing(b):
                yield from route_norm(b)
                for j in range(TPB):
                    yield from route(b * TPB + j)

            def tower(b, before, now):
                run = lambda there, n, stage, *args: stage(*args) if there else idle(n)
                yield from run(before, ATTEND_STEPS, attend, b - 1, TPB - 1, (ao_h, b * TPB - 1))
                yield from run(before, GATES_STEPS, gates, b - 1)
                yield from run(before, DIRECTION_STEPS, direction, b - 1, 0, b * TPB)
                yield from run(now, ATTEND_STEPS, attend, b, 0, (y_in, count(2 * b - 1)))
                yield from run(before, DIRECTION_STEPS, direction, b - 1, 1, b * TPB + now)
                yield from run(before, OUT_STEPS, mix_out, b - 1)
                yield from run(now, ATTEND_STEPS, attend, b, 1, (m_done, b))
                yield from run(before, EXPERTS_STEPS, experts, b - 1)
                yield from run(now, ATTEND_STEPS, attend, b, 2, (y2_read, b * TPB))

            def batch(b, before=True, more=True):
                lines = [(tower(b, before, True), TOWER_STEPS)]
                if more:
                    lines.append((routing(b + 1), ROUTING_STEPS))
                units = TPB * HEADS
                for u in range(units):
                    j, hd = divmod(u, HEADS)
                    if u % 2 == 0 and (before or u > 0):
                        turn_kT(*((b, j, hd // 2 - 1) if hd > 0 else (b, j - 1, 3) if j > 0 else (b - 1, TPB - 1, 3)))
                    weigh(b * TPB + j, hd)
                    for line, steps in lines:
                        for _ in range(steps * (u + 1) // units - steps * u // units):
                            next(line)
                    add_up(b, j, hd)
                for line, _ in lines:
                    for _ in line:
                        assert False, "steps are missing in a line's count"

            for _ in routing(0):
                pass
            batch(0, before=False)
            with eng.Fori(1, B - 1) as b:
                batch(b)
            batch(B - 1, more=False)
            turn_kT(B - 1, TPB - 1, 3)
            for _ in tower(B, True, False):
                pass

        settled = {}

        def settle(eng):
            if eng not in settled:
                settled[eng] = sem(f"settled{len(settled)}")
            eng.sem_inc(settled[eng], 1)

        def bc(ap, shape, axis):
            return ap.unsqueeze(axis).broadcast_to(shape)

        n_loads = []

        @block.sync
        def _(sp):

            def load(dst, src):
                sp.dma_start(dst, src).then_inc(loaded, 16)
                n_loads.append(1)

            sp.wait_ge(ids_zeroed, 1)
            for g in range(GROUPS):
                for p, name in enumerate(("x", "itok_BS_0_23", "itok_BS_0_11", "itok_BS_0_30")):
                    src = A[name].rearrange("b s -> (b s)")[g * GTOK:(g + 1) * GTOK]
                    first = 32 * g + 2 * HARM * p
                    sp.dma_start(idsb[first:first + 2 * HARM, :], bc(src, [2 * HARM, GTOK], 0)).then_inc(ids_in, 16)
            for g in range(GROUPS):
                r = slice(32 * g, 32 * g + FD)
                load(w_feat[r, 0:3], A["feature_constants"])
                load(w_feat[r, 3:4], A["hw_by_feature"])
                load(w_feat[r, 4:5], A["ph_by_feature"])
                load(tW1[r, :], A["L0_tok_W1"])
                load(tWres[r, :], A["L0_tok_Wres"])
            load(tW2[:], A["L0_tok_W2"])
            load(tb1[:], A["L0_tok_b1"].unsqueeze(1))
            for i, name in enumerate(("L0_tok_b2", "L0_tok_gamma", "L0_tok_beta", "L0_tok_bres")):
                load(trow[:, i, :], bc(A[name], [P, D], 0))
            load(wqpk[:], A["L0_ffn_Wq_pk"])
            load(wq[:], A["L0_ffn_Wq"])
            load(wo[:], A["L0_ffn_Wo"].rearrange("(c p) n -> p c n", p=P))
            load(winT[:], A["W_inT"])
            load(wgT[:], A["W_gT"].rearrange("(c p) n -> p c n", p=P))
            load(bg_m[:], A["b_gT"])
            sp.wait_ge(weights_zeroed, 1)
            for d, s in enumerate("fb"):
                load(wxpT[:, d, 0:RANK], A["W_xpT_" + s][:, 0:RANK])
                for i in range(1, 4):
                    load(wxpT[:, d, 2 * NST * i:2 * NST * (i + 1)], A["W_xpT_" + s][:, RANK:RANK + 2 * NST])
                load(wdtT[:, d, :], A["W_dtT_" + s])
                load(bdt[:, d:d + 1], A["L1_attn_b_dt_" + s].unsqueeze(1))
                load(negA[:, d, :], A["L1_attn_A_log_" + s])
                load(Dskip[:, d:d + 1], A["L1_attn_D_" + s].unsqueeze(1))
            load(woutT[:], A["W_outT"].rearrange("(c p) n -> p c n", p=P))
            load(eWg[:], A["L1_ffn_Wg"])
            load(ebias[:, 0, :], bc(A["L1_ffn_bg"], [P, EXP], 0))
            load(ebias[:, 1, :], bc(A["L1_ffn_bias"], [P, EXP], 0))
            load(eW1[:], A["L1_ffn_W1"].rearrange("e d f -> d e f"))
            load(eb1[:], A["eb1T"])
            load(eW2[:], A["L1_ffn_W2"].rearrange("e f d -> f e d"))
            load(eb2[:], A["L1_ffn_b2"].rearrange("e d -> (e d)").unsqueeze(0))
            for g in range(4):
                load(keys[32 * g:32 * g + 32, :, NKEY * g:NKEY * g + NKEY],
                     A["keysT"].rearrange("(c g) d k -> g d c k", g=4)[g])
            out_v = out.rearrange("b s d -> (b s) d").rearrange("(t p) d -> p t d", p=P)
            with sp.Fori(0, B) as b:
                sp.wait_ge(e_done, b + 1)
                sp.dma_start(out_v[:, bass.ds(b * TPB, TPB), :], hout[:]).then_inc(stored, 16)
                sp.wait_ge(stored, 16 * b + 16)
                settle(sp)

        LOADS = len(n_loads)

        @block.gpsimd
        def _(pool):
            pool.memset(idf[:], 0.0)
            pool.memset(idb[:], 0.0)
            pool.memset(causal[:], 0.0)
            pool.memset(ones[:], 1.0)
            pool.memset(wxpT[:], 0.0)
            pool.memset(qz[:], 0.0)
            pool.memset(keys[:], 0.0).then_inc(weights_zeroed, 1)
            pool.drain()
            pool.affine_select(out=idf[:], in_=idf[:], compare_op=ALU.not_equal, fill=1.0, base=0,
                               pattern=[[-1, P]], channel_multiplier=1)
            pool.affine_select(out=idb[:], in_=idb[:], compare_op=ALU.not_equal, fill=1.0, base=0,
                               pattern=[[-1, P]], channel_multiplier=1)
            pool.affine_select(out=causal[:], in_=causal[:], compare_op=ALU.is_ge, fill=-1e30, base=0,
                               pattern=[[-1, P]], channel_multiplier=1)
            pool.iota(cand_no[:], pattern=[[1, NCAND]], base=0, channel_multiplier=0,
                      allow_small_or_imprecise_dtypes=True)
            pool.iota(exp_no[:], pattern=[[1, EXP]], base=0, channel_multiplier=0,
                      allow_small_or_imprecise_dtypes=True)
            pool.iota(head_base[:], pattern=[[NKEY * NKEY, HEADS], [0, TOPK]], base=0, channel_multiplier=0,
                      allow_small_or_imprecise_dtypes=True).then_inc(consts, 1)
            with pool.Fori(0, TILES // 2) as t2:
                for u in range(2):
                    t = t2 * 2 + u
                    pool.wait_ge(ids_ready, t + 1)
                    pool.tensor_copy(ids_now[:, u, :], ids_ring[:, t % RING, :])
                    pool.drain()
                    for hd in range(HEADS):
                        pool.wait_ge(summed, t * HEADS + hd + 1)
                        settle(pool)
                        for k in range(TOPK):
                            c = hd * TOPK + k
                            pool.indirect_dma_start(
                                rows[:, hd % SLOTS, k, :], None, A["kv_table"],
                                bass.IndirectOffsetOnAxis(ap=ids_now[:, u, c:c + 1], axis=0),
                            ).then_inc(landed[hd % SLOTS], 16)

        @block.tensor
        def _(pe):
            mm = pe.matmul
            pe.wait_ge(loaded, 16 * LOADS)
            pe.wait_ge(consts, 1)

            with pe.Fori(0, 2) as c:
                pe.wait_ge(chunk_in, c + 1)
                for g in range(GROUPS):
                    r = slice(32 * g, 32 * g + FD)
                    n = c * GROUPS + g
                    mm(bank[g % 2][:, :], tW1[r, :], feat_now[r, :], start=True, stop=True).then_inc(h1_ps, 1)
                    pe.wait_ge(h1_sb, n + 1)
                    pe.wait_ge(h2_read, n)
                    for j in range(TPB):
                        t = slice(P * j, P * j + P)
                        mm(bank[2][:, D * j:D * j + D], h1[:, g % 2, t], tW2[:], start=True, stop=True)
                        last = mm(bank[2][:, 256 + D * j:256 + D * j + D], feat_now[r, t], tWres[r, :],
                                  start=True, stop=True)
                    last.then_inc(h2_ps, 1)

            with pe.Fori(0, B) as b:
                pe.wait_ge(f_done, b + 1)
                settle(pe)
                for j in range(TPB):
                    last = pe.transpose(bank[3][0:D, P * j:P * j + P], NM["sq"][:, j, :], idf[:])
                last.then_inc(fT_ps, 1)
                pe.wait_ge(fT_sb, b + 1)

            pe.wait_ge(f1_in, B)
            with pe.Fori(0, B) as b:
                n = b * TILES

                def mix(j):
                    pe.wait_ge(score_exp, n + j + 1)
                    if j == 0:
                        pe.wait_ge(mix_sb, b)
                    i = mm(bank[3][0:D + 1, :], f1[:, j, :], esc[:, j % 3, :], start=(j == 0), stop=(j == TILES - 1))
                    if j == TILES - 1:
                        i.then_inc(mix_ps, 1)
                    else:
                        i.then_inc(mixed, 1)

                for j in range(TILES):
                    if j >= 3:
                        pe.wait_ge(score_exp, n + j - 2)
                        settle(pe)
                    mm(bank[j % 3][:, :], fT[:, P * j:P * j + P], fT[:, bass.ds(b * S, S)],
                       start=True, stop=True).then_inc(score_ps, 1)
                    if j >= 2:
                        mix(j - 2)
                mix(TILES - 2)
                mix(TILES - 1)
                pe.wait_ge(mix_sb, b + 1)
                pe.wait_ge(mixT_read, b)
                for j in range(TPB):
                    last = pe.transpose(bank[4][:, (D + 1) * j:(D + 1) * (j + 1)], uT[:, P * j:P * j + P],
                                        idf[0:D + 1, 0:D + 1])
                last.then_inc(mixT_ps, 1)

            def turn_kT(b, j, c):
                p = (b * TPB + j) * 4 + c
                pe.wait_ge(kv_sb, 2 * p + 2)
                pe.transpose(bank[3][:, 0:P], k_now[:, P * c:P * c + P], idf[:]).then_inc(kT_ps, 1)

            def weigh(t, hd):
                pass

            def add_up(b, j, hd):
                m = (b * TPB + j) * HEADS + hd
                pe.wait_ge(weighted, m + 1)
                pe.wait_ge(kv_sb, count(m - 1))
                if hd % 2 == 1:
                    pe.wait_ge(kT_sb, count((b * TPB + j) * 4 + hd // 2))
                for k in range(TOPK):
                    last = mm(bank[3 * (hd % 2)][:, 0:2 * D], idf[:], rows[:, hd % SLOTS, k, :],
                              start=(k == 0), stop=(k == TOPK - 1))
                last.then_inc(summed, 1)

            def route_norm(b):
                yield from idle(2)
                pe.wait_ge(r_x, b + 1)
                pe.wait_ge(sim_sb, b * TPB)
                settle(pe)
                for j in range(TPB):
                    last = pe.transpose(bank[1][0:D, P * j:P * j + P], NR["sq"][:, j, :], idf[:])
                last.then_inc(r_xT_ps, 1)
                yield

            def route(t):
                pe.wait_ge(r_xT, t // TPB + 1)
                pe.wait_ge(sim_sb, t)
                settle(pe)
                for c in range(4):
                    last = mm(bank[1][:, P * c:P * c + P], wqpk[:, P * c:P * c + P],
                              xT[:, bass.ds((t % (XRING * TPB)) * P, P)], start=True, stop=True)
                last.then_inc(q_ps, 1)
                yield
                pe.wait_ge(q_sb, t + 1)
                for c in range(4):
                    last = mm(bank[1 + c // 2][:, 256 * (c % 2):256 * (c % 2) + 256], qpkT[:, c, :], keys[:, c, :],
                              start=True, stop=True)
                last.then_inc(sim_ps, 1)
                yield from idle(ROUTE_STEPS - 1)

            def attend(b, i, free):
                par = b % 2
                t = b * TPB + i
                g = t * HEADS

                def scores(u):
                    pe.wait_ge(a_exp, count(g + u - 1))
                    ps = bank[4 + u % 2]
                    mm(ps[:, 0:P * (i + 1)], qz[:, u, :], kT[:, par, u // 2, 0:P * (i + 1)], start=True, stop=False)
                    mm(ps[:, P * i:P * i + P], idb[:], causal[:], start=False, stop=True).then_inc(a_s, 1)

                def turn_probs(u):
                    pe.wait_ge(a_exp, g + u + 1)
                    pe.wait_ge(a_Tsb, g + u)
                    for j in range(i + 1):
                        last = pe.transpose(bank[6][:, P * j:P * j + P], prob[:, u % 2, P * j:P * j + P], idf[:])
                    last.then_inc(a_T, 1)

                def mix_values(u):
                    pe.wait_ge(a_Tsb, g + u + 1)
                    pe.wait_ge(a_norm, g + u)
                    for j in range(i + 1):
                        last = mm(bank[7][:, 0:D], probT[:, u % 2, j, :], val[:, par, j, u, :],
                                  start=(j == 0), stop=(j == i))
                    last.then_inc(a_o, 1)

                pe.wait_ge(free[0], free[1])
                pe.wait_ge(kT_sb, 4 * t + 4)
                settle(pe)
                for c in range(4):
                    last = mm(bank[6][:, P * c:P * c + P], wq[:, P * c:P * c + P],
                              xT[:, bass.ds((t % (XRING * TPB)) * P, P)], start=True, stop=True)
                last.then_inc(aq_ps, 1)
                yield
                pe.wait_ge(aq_sb, t + 1)
                scores(0)
                yield
                for u in range(HEADS):
                    if u + 1 < HEADS:
                        scores(u + 1)
                    turn_probs(u)
                    if u > 0:
                        mix_values(u - 1)
                    yield
                mix_values(HEADS - 1)
                yield
                pe.wait_ge(a_norm, g + HEADS)
                for c in range(4):
                    last = pe.transpose(bank[6][:, P * c:P * c + P], o_now[:, P * c:P * c + P], idf[:])
                last.then_inc(ao_T, 1)
                yield
                pe.wait_ge(ao_sb, t + 1)
                for c in range(4):
                    last = mm(bank[7][:, 0:D], oT[:, c, :], wo[:, c, :], start=(c == 0), stop=(c == 3))
                last.then_inc(ao_ps, 1)
                yield

            def gates(b):
                yield from idle(2)
                pe.wait_ge(m_x, b + 1)
                settle(pe)
                for j in range(TPB):
                    last = pe.transpose(bank[4][0:D, P * j:P * j + P], NM["sq"][:, j, :], idf[:])
                last.then_inc(m_xT_ps, 1)
                yield
                pe.wait_ge(m_xT, b + 1)
                for c in range(4):
                    mm(bank[4 + (c + 1) % 4][:, :], winT[:, P * c:P * c + P], xt4, start=True,
                       stop=True).then_inc(xz_ps, 1)
                yield
                pe.wait_ge(mean_in, b + 1)
                for m in range(4):
                    for k in range(4):
                        last = mm(bank[5][:, m:m + 1], wgT[:, k, P * m:P * m + P], xmean[:, k:k + 1],
                                  start=(k == 0), stop=(k == 3))
                last.then_inc(gsh_ps, 1)
                yield from idle(GATES_STEPS - 4)

            def direction(b, d, tiles):
                m = b * 2 + d
                n0 = m * NST

                def spread_B(n):
                    if n >= 2:
                        pe.wait_ge(dBu_in, n0 + n - 1)
                    mm(bank[4 + 2 * (n % 2)][:, :], spread3[:, n:n + 1].broadcast_to([P, P]), bc3[:],
                       start=True, stop=True).then_inc(B_ps, 1)

                def spread_C(n):
                    if n >= 1:
                        pe.wait_ge(hC_in, n0 + n)
                    mm(bank[5][:, :], spread3[:, NST + n:NST + n + 1].broadcast_to([P, P]), bc3[:],
                       start=True, stop=True).then_inc(C_ps, 1)

                def add_y(n):
                    pe.wait_ge(hC_in, n0 + n + 1)
                    mm(bank[7][:, :], idf[:], hC[:, n % 2, :], start=(n == 0), stop=(n == NST - 1)).then_inc(y_ps, 1)

                pe.wait_ge(act_in, b + 1)
                mm(bank[6][:, :], wxpT[:, d, :], xz[:, 2 * d, :], start=True, stop=True).then_inc(xd_ps, 1)
                yield
                pe.wait_ge(ao_h, tiles)
                if d == 1:
                    pe.wait_ge(y_in, m)
                pe.wait_ge(xd_sb, m + 1)
                mm(bank[7][:, :], wdtT[:, d, :], dt_low, start=True, stop=True).then_inc(dt_ps, 1)
                yield
                yield
                pe.wait_ge(bc_in, m + 1)
                spread_B(0)
                pe.wait_ge(sp_e, m + 1)
                yield
                for n in range(NST):
                    spread_C(n)
                    if n + 1 < NST:
                        spread_B(n + 1)
                    if n > 0:
                        add_y(n - 1)
                    yield
                add_y(NST - 1)
                yield from idle(2)

            def mix_out(b):
                pe.wait_ge(y_in, 2 * b + 2)
                for j in range(TPB):
                    for d in range(2):
                        last = mm(bank[6][:, D * j:D * j + D], gate[:, 2 * d, P * j:P * j + P], woutT[:, d, :],
                                  start=(d == 0), stop=(d == 1))
                last.then_inc(m_out_ps, 1)
                yield from idle(OUT_STEPS)

            def experts(b):
                yield from idle(2)
                pe.wait_ge(e_x, b + 1)
                settle(pe)
                for j in range(TPB):
                    last = pe.transpose(bank[4][0:D, P * j:P * j + P], NM["sq"][:, j, :], idf[:])
                last.then_inc(e_xT_ps, 1)
                yield
                pe.wait_ge(e_xT, b + 1)
                for j in range(TPB):
                    last = mm(bank[5][:, EXP * j:EXP * j + EXP], xt4[:, P * j:P * j + P], eWg[:], start=True, stop=True)
                last.then_inc(lg_ps, 1)
                for e in range(EXP):
                    if e >= 2:
                        pe.wait_ge(hid_sb, EXP * b + e - 1)
                    mm(bank[6 + e % 2][:, :], eW1[:, e, :], xt4, start=True, stop=True).then_inc(hid_ps, 1)
                    if e % 2 == 1:
                        yield
                pe.wait_ge(lg_read, b + 1)
                pe.wait_ge(hid_sb, EXP * b + EXP)
                for j in range(TPB):
                    ps = bank[4 + j % 2]
                    if j >= 2:
                        pe.wait_ge(y2_read, TPB * b + j - 1)
                    mm(ps[:, :], ones[:], eb2[:], start=True, stop=False)
                    for e in range(EXP):
                        last = mm(ps[:, D * e:D * e + D], hid[:, e, P * j:P * j + P], eW2[:, e, :],
                                  start=False, stop=(e == EXP - 1))
                    last.then_inc(y2_ps, 1)
                    yield
                yield

            schedule(pe, (turn_kT, weigh, add_up), route_norm, route, attend, gates, direction, mix_out, experts)

        @block.scalar
        def _(act):
            ac = act.activation
            act.wait_ge(consts, 1)

            def rstd(N, done_v, done_r, n, scale=1.0):
                act.wait_ge(done_v, n + 1)
                ac(N["l"][:], N["v"][:], ACT.Ln, scale=scale)
                act.drain()
                ac(N["y0"][:], N["l"][:], ACT.Exp, scale=-0.5).then_inc(done_r, 1)

            act.wait_ge(angle_done, 1)
            ac(feat, ang, ACT.Sin).then_inc(feat_done, 1)
            act.preload_act_table_set("natural_log_exp_and_others")
            act.wait_ge(loaded, 16 * LOADS)
            ac(negA[:], negA[:], ACT.Exp)
            act.drain()
            ac(negA[:], negA[:], ACT.Copy, scale=-1.0)
            with act.Fori(0, 2) as c:
                for g in range(GROUPS):
                    n = c * GROUPS + g
                    act.wait_ge(h1_ps, n + 1)
                    ac(h1[:, g % 2, :], bank[g % 2][:, :], ACT.Relu, bias=tb1[:, 0:1]).then_inc(h1_sb, 1)
                    rstd(NM, t_var, t_rstd, n)
            with act.Fori(0, B) as b:
                rstd(NM, u_var, u_rstd, b)
                rstd(NM, u_sq, u_rl2, b, scale=2.0 ** 40)
                act.wait_ge(fT_ps, b + 1)
                ac(fT[:, bass.ds(b * S, S)], bank[3][0:D, :], ACT.Copy).then_inc(fT_sb, 1)
            with act.Fori(0, B) as b:
                n = b * TILES
                for j in range(TILES):
                    act.wait_ge(score_ps, n + j + 1)
                    if j >= 3:
                        act.wait_ge(mixed, b * (TILES - 1) + j - 2)
                    else:
                        act.wait_ge(mix_ps, b)
                    ac(esc[:, j % 3, :], bank[j % 3][:, :], ACT.Exp).then_inc(score_exp, 1)
                act.wait_ge(mix_ps, b + 1)
                act.wait_ge(mixT_ps, b)
                ac(uT, bank[3][0:D + 1, :], ACT.Copy).then_inc(mix_sb, 1)
                rstd(NM, m_sq, m_rl2, b, scale=2.0 ** 40)

            def turn_kT(b, j, c):
                p = (b * TPB + j) * 4 + c
                act.wait_ge(kT_ps, p + 1)
                ac(kT[:, b % 2, c, P * j:P * j + P], bank[3][:, 0:P], ACT.Copy).then_inc(kT_sb, 1)

            def weigh(t, hd):
                pass

            def add_up(b, j, hd):
                m = (b * TPB + j) * HEADS + hd
                ps = bank[3 * (hd % 2)]
                act.wait_ge(summed, SLOTS + m + 1)
                ac(k_now[:, D * hd:D * hd + D], ps[:, 0:D], ACT.Copy)
                ac(val[:, b % 2, j, hd, :], ps[:, D:2 * D], ACT.Copy).then_inc(kv_sb, 1)

            def route_norm(b):
                rstd(NR, r_var, r_rstd, b)
                yield from idle(2)
                act.wait_ge(r_xT_ps, b + 1)
                ac(xT[:, bass.ds((b % XRING) * S, S)], bank[1][0:D, :], ACT.Copy).then_inc(r_xT, 1)
                yield

            def route(t):
                act.wait_ge(q_ps, t + 1)
                ac(qpkT[:, :, :].rearrange("p c t -> p (c t)"), bank[1][:, :], ACT.Copy).then_inc(q_sb, 1)
                yield
                act.wait_ge(sim_ps, t + 1)
                act.wait_ge(picked, t)
                for i in range(2):
                    last = ac(sim[:, 8 * i:8 * i + 8, :].rearrange("p r k -> p (r k)"), bank[1 + i][:, :], ACT.Copy)
                last.then_inc(sim_sb, 1)
                yield from idle(5)
                act.wait_ge(shifted, t + 1)
                ac(shift[:], shift[:], ACT.Exp).then_inc(exped, 1)
                yield from idle(6)

            def attend(b, i, free):
                t = b * TPB + i
                g = t * HEADS

                def expo(u):
                    w = P * (i + 1)
                    act.wait_ge(a_max, g + u + 1)
                    ac(prob[:, u % 2, 0:w], bank[4 + u % 2][:, 0:w], ACT.Exp, bias=negmax[:, u % 2:u % 2 + 1],
                       accum_out=psum_row[:, u % 4:u % 4 + 1]).then_inc(a_exp, 1)

                act.wait_ge(aq_ps, t + 1)
                for half in range(2):
                    r = slice(D * half, D * half + D)
                    last = ac(qz[r, half::2, :], bank[6][r, :].rearrange("p (c t) -> p c t", t=P), ACT.Copy,
                              scale=D ** -0.5)
                last.then_inc(aq_sb, 1)
                yield
                expo(0)
                yield
                for u in range(HEADS):
                    if u + 1 < HEADS:
                        expo(u + 1)
                    act.wait_ge(a_T, g + u + 1)
                    act.wait_ge(a_o, count(g + u - 1))
                    ac(probT[:, u % 2, 0:i + 1, :], bank[6][:, 0:P * (i + 1)].rearrange("p (c t) -> p c t", t=P),
                       ACT.Copy).then_inc(a_Tsb, 1)
                    yield
                yield
                act.wait_ge(ao_T, t + 1)
                ac(oT[:], bank[6][:, :].rearrange("p (c t) -> p c t", t=P), ACT.Copy).then_inc(ao_sb, 1)
                yield
                yield

            def gates(b):
                rstd(NM, m_var, m_rstd, b)
                yield from idle(2)
                act.wait_ge(m_xT_ps, b + 1)
                ac(xt4, bank[4][0:D, :], ACT.Copy).then_inc(m_xT, 1)
                yield
                for c in range(4):
                    act.wait_ge(xz_ps, 4 * b + c + 1)
                    ac(xz[:, c, :], bank[4 + (c + 1) % 4][:, :], ACT.Copy, accum_out=xsum[:, c:c + 1]).then_inc(xz_sb, 1)
                yield from idle(2)
                act.wait_ge(gsh_in, b + 1)
                for c in range(4):
                    last = ac(gate[:, c, :], xz[:, c, :], ACT.Exp, bias=ngsh[:, c:c + 1], scale=-1.0)
                last.then_inc(sig_e, 1)
                yield from idle(3)

            def direction(b, d, tiles):
                m = b * 2 + d
                n0 = m * NST

                def decay(n):
                    if n >= 2:
                        act.wait_ge(scanned, n0 + n - 1)
                    ac(dA[:, n % 2, :], dt[:], ACT.Exp, scale=negA[:, d, n:n + 1]).then_inc(dA_in, 1)

                act.wait_ge(xd_ps, m + 1)
                ac(bc3[:], bank[6][:, :], ACT.Copy)
                ac(dt_low, bank[6][0:RANK, :], ACT.Copy).then_inc(xd_sb, 1)
                yield
                act.wait_ge(dt_ps, m + 1)
                ac(sp_relu, bank[7][:, :], ACT.Relu, bias=bdt[:, d:d + 1])
                ac(sp_w, bank[7][:, :], ACT.Abs, bias=bdt[:, d:d + 1])
                act.drain()
                ac(sp_u, sp_w, ACT.Exp, scale=-1.0).then_inc(sp_e, 1)
                yield from idle(2)
                act.wait_ge(dt_in, m + 1)
                decay(0)
                yield
                for n in range(NST):
                    if n + 1 < NST:
                        decay(n + 1)
                    yield
                yield from idle(2)

            def mix_out(b):
                yield from idle(OUT_STEPS)

            def experts(b):
                rstd(NM, e_var, e_rstd, b)
                yield from idle(2)
                act.wait_ge(e_xT_ps, b + 1)
                ac(xt4, bank[4][0:D, :], ACT.Copy).then_inc(e_xT, 1)
                yield
                act.wait_ge(m_done, b + 1)
                for e in range(EXP):
                    act.wait_ge(hid_ps, EXP * b + e + 1)
                    ac(hid[:, e, :], bank[6 + e % 2][:, :], ACT.Relu, bias=eb1[:, e:e + 1]).then_inc(hid_sb, 1)
                    if e == 3:
                        act.wait_ge(top_d, b + 1)
                        ac(tw[:, 1, :], tw[:, 0, :], ACT.Exp).then_inc(top_e, 1)
                    if e % 2 == 1:
                        yield
                yield from idle(5)

            schedule(act, (turn_kT, weigh, add_up), route_norm, route, attend, gates, direction, mix_out, experts)

        @block.vector
        def _(dve):
            tt, ts, stt = dve.tensor_tensor, dve.tensor_scalar, dve.scalar_tensor_tensor

            def seq(*ops):
                for i, op in enumerate(ops):
                    last = op()
                    if i + 1 < len(ops):
                        dve.drain()
                return last

            def newton(N, v):
                return (lambda: tt(N["t"][:], N["y0"][:], N["y0"][:], ALU.mult),
                        lambda: tt(N["t"][:], N["t"][:], v, ALU.mult),
                        lambda: ts(N["t"][:], N["t"][:], -0.5, 1.5, ALU.mult, ALU.add),
                        lambda: tt(N["r"][:], N["t"][:], N["y0"][:], ALU.mult))

            def centre(N, src, done_v):
                seq(lambda: dve.tensor_reduce(N["s"][:], src, AX.X, ALU.add),
                    lambda: stt(out=N["xc"][:], in0=bc(N["s"][:], [P, TPB, D], 2), scalar=-1.0 / D, in1=src,
                                op0=ALU.mult, op1=ALU.add),
                    lambda: tt(N["sq"][:], N["xc"][:], N["xc"][:], ALU.mult),
                    lambda: dve.tensor_reduce(N["s"][:], N["sq"][:], AX.X, ALU.add),
                    lambda: ts(N["v"][:], N["s"][:], 1.0 / D, EPS, ALU.mult, ALU.add).then_inc(done_v, 1))

            def scaled(N, done_r, n):
                dve.wait_ge(done_r, n + 1)
                return seq(*newton(N, N["v"][:]),
                           lambda: tt(N["sq"][:], N["xc"][:], bc(N["r"][:], [P, TPB, D], 2), ALU.mult))

            dve.memset(w_feat[:], 0.0)
            dve.memset(idsb, 0).then_inc(ids_zeroed, 1)
            dve.memset(f1[:, :, D:D + 1], 1.0)
            dve.wait_ge(consts, 1)
            dve.wait_ge(ids_in, 16 * GROUPS * NPER)
            dve.wait_ge(loaded, 16 * LOADS)
            col = [w_feat[:, i:i + 1] for i in range(5)]
            seq(lambda: dve.tensor_copy(ang, idsb),
                lambda: ts(ang, ang, TWO_PI, col[0], ALU.mult, ALU.mult),
                lambda: ts(ang, ang, col[1], col[4], ALU.mult, ALU.add),
                lambda: ts(turn, ang, col[2], 1.0 / TWO_PI, ALU.add, ALU.mult),
                lambda: ts(turn, turn, ROUND, -ROUND, ALU.add, ALU.add),
                lambda: stt(out=ang, in0=turn, scalar=-PI_A, in1=ang, op0=ALU.mult, op1=ALU.add),
                lambda: stt(out=ang, in0=turn, scalar=-PI_B, in1=ang, op0=ALU.mult, op1=ALU.add),
                lambda: stt(out=ang, in0=turn, scalar=-PI_C, in1=ang, op0=ALU.mult, op1=ALU.add),
                lambda: ts(ang, ang, col[2], PI_MAX, ALU.add, ALU.min),
                lambda: ts(ang, ang, -PI_MAX, None, ALU.max).then_inc(angle_done, 1))
            dve.wait_ge(feat_done, 1)
            ts(feat, feat, col[3], None, ALU.mult)
            with dve.Fori(0, 2) as c:
                dve.drain()
                dve.wait_ge(h2_ps, c * GROUPS)
                dve.tensor_copy(feat_now, feat[:, bass.ds(c * S, S)]).then_inc(chunk_in, 1)
                for g in range(GROUPS):
                    n = c * GROUPS + g
                    dve.drain()
                    dve.wait_ge(h2_ps, n + 1)
                    h2 = bank[2][:, 0:256].rearrange("p (j d) -> p j d", d=D)
                    res = bank[2][:, 256:512].rearrange("p (j d) -> p j d", d=D)
                    row = [bc(trow[:, i, :], [P, TPB, D], 1) for i in range(4)]
                    dst = h[:, bass.ds(c * TPB + g * (GTOK // P), TPB), :]
                    tt(ymix[:], h2, row[0], ALU.add)
                    tt(hout[:], res, row[3], ALU.add).then_inc(h2_read, 1)
                    dve.drain()
                    centre(NM, ymix[:], t_var)
                    scaled(NM, t_rstd, n)
                    dve.drain()
                    seq(lambda: tt(NM["sq"][:], NM["sq"][:], row[1], ALU.mult),
                        lambda: tt(NM["sq"][:], NM["sq"][:], row[2], ALU.add),
                        lambda: stt(out=dst, in0=hout[:], scalar=0.1, in1=NM["sq"][:], op0=ALU.mult, op1=ALU.add))
            dve.drain()

            with dve.Fori(0, B) as b:
                tile4 = bass.ds(b * TPB, TPB)
                dve.wait_ge(fT_ps, b)
                centre(NM, h[:, tile4, :], u_var)
                dve.wait_ge(u_rstd, b + 1)
                seq(*newton(NM, NM["v"][:]),
                    lambda: tt(tw[:, 0, :], NM["r"][:], NM["r"][:], ALU.mult),
                    lambda: tt(tw[:, 0, :], tw[:, 0, :], NM["s"][:], ALU.mult),
                    lambda: ts(NM["v"][:], tw[:, 0, :], 1e-24, None, ALU.max).then_inc(u_sq, 1))
                dve.tensor_copy(tw[:, 1, :], NM["r"][:])
                dve.wait_ge(u_rl2, b + 1)
                seq(lambda: ts(NM["y0"][:], NM["y0"][:], 2.0 ** 20, None, ALU.mult),
                    *newton(NM, NM["v"][:]),
                    lambda: tt(NM["r"][:], NM["r"][:], tw[:, 1, :], ALU.mult),
                    lambda: tt(NM["sq"][:], NM["xc"][:], bc(NM["r"][:], [P, TPB, D], 2), ALU.mult).then_inc(f_done, 1),
                    lambda: dve.tensor_copy(f1[:, tile4, 0:D], NM["sq"][:]).then_inc(f1_in, 1))
                dve.drain()

            with dve.Fori(0, B) as b:
                tile4 = bass.ds(b * TPB, TPB)
                dve.wait_ge(mixT_ps, b + 1)
                mixT = bank[4][:, 0:TPB * (D + 1)].rearrange("p (j d) -> p j d", d=D + 1)
                seq(lambda: dve.reciprocal(tw[:, 0, :].unsqueeze(2), mixT[:, :, D:D + 1]),
                    lambda: ts(tw[:, 0, :], tw[:, 0, :], 1.0 - 0.8, None, ALU.mult),
                    lambda: tt(NM["xc"][:], mixT[:, :, 0:D], bc(tw[:, 0, :], [P, TPB, D], 2),
                               ALU.mult).then_inc(mixT_read, 1),
                    lambda: stt(out=NM["xc"][:], in0=f1[:, tile4, 0:D], scalar=0.8, in1=NM["xc"][:],
                                op0=ALU.mult, op1=ALU.add),
                    lambda: tt(NM["sq"][:], NM["xc"][:], NM["xc"][:], ALU.mult),
                    lambda: dve.tensor_reduce(NM["s"][:], NM["sq"][:], AX.X, ALU.add),
                    lambda: ts(NM["v"][:], NM["s"][:], 1e-24, None, ALU.max).then_inc(m_sq, 1))
                dve.wait_ge(m_rl2, b + 1)
                seq(lambda: ts(NM["y0"][:], NM["y0"][:], 2.0 ** 20, None, ALU.mult),
                    *newton(NM, NM["v"][:]),
                    lambda: tt(NM["xc"][:], NM["xc"][:], bc(NM["r"][:], [P, TPB, D], 2), ALU.mult),
                    lambda: tt(h[:, tile4, :], h[:, tile4, :], NM["xc"][:], ALU.add))
                dve.drain()
            dve.memset(fsum[:], 0.0).then_inc(summed, SLOTS)

            tt(spread3[:], idb[:, 32:64], idb[:, 64:96], ALU.add)
            dve.drain()
            tt(spread3[:], spread3[:], idb[:, 96:128], ALU.add)
            dve.drain()

            def turn_kT(b, j, c):
                pass

            def add_up(b, j, hd):
                pass

            def weigh(t, hd):
                slot = hd % SLOTS
                dve.wait_ge(landed[slot], 16 * TOPK * (t * (HEADS // SLOTS) + hd // SLOTS + 1))
                tt(rows[:, slot, :, :], rows[:, slot, :, :],
                   bc(w_ring[:, t % RING, TOPK * hd:TOPK * hd + TOPK], [P, TOPK, 2 * D], 2),
                   ALU.mult).then_inc(weighted, 1)

            def route_norm(b):
                dve.wait_ge(r_xT_ps, b)
                centre(NR, h[:, bass.ds(b * TPB, TPB), :], r_var)
                yield
                scaled(NR, r_rstd, b).then_inc(r_x, 1)
                yield
                yield

            def route(t):
                ring = t % RING
                yield from idle(2)
                dve.wait_ge(sim_sb, t + 1)
                settle(dve)
                rr = range(ROWS)
                for r in rr:
                    dve.max(best[:, r, 0:8], sim[:, r, :])
                dve.drain()
                yield
                for r in rr:
                    dve.match_replace(sim2[:, r, :], best[:, r, 0:8], sim[:, r, :], LOW)
                    last = dve.max_index(besti[:, r, 0:8], best[:, r, 0:8], sim[:, r, :])
                last.then_inc(picked, 1)
                dve.drain()
                yield
                for r in rr:
                    dve.max(best[:, r, 8:16], sim2[:, r, :])
                dve.drain()
                for r in rr:
                    dve.max_index(besti[:, r, 8:16], best[:, r, 8:16], sim2[:, r, :])
                dve.drain()
                tt(bestf[:, 0:HEADS, :], besti[:, 0:HEADS, :], head_base[:], ALU.add)
                ts(bestf[:, HEADS:ROWS, :], besti[:, HEADS:ROWS, :], float(NKEY), None, ALU.mult)
                dve.drain()
                yield
                for src, dst in ((best, cval), (bestf, cid)):
                    at = 0
                    for a in range(WIDE):
                        n = CAND[a]
                        tt(dst[:, :, at:at + n], src[:, 0:HEADS, a:a + 1].broadcast_to([P, HEADS, n]),
                           src[:, HEADS:ROWS, 0:n], ALU.add)
                        at += n
                    n = TOPK - WIDE
                    tt(dst[:, :, at:at + n], src[:, 0:HEADS, WIDE:TOPK],
                       src[:, HEADS:ROWS, 0:1].broadcast_to([P, HEADS, n]), ALU.add)
                dve.drain()
                hh = range(HEADS)
                for r in hh:
                    dve.max(fval[:, r, 0:8], cval[:, r, :])
                dve.drain()
                yield
                for r in hh:
                    dve.match_replace(cval2[:, r, :], fval[:, r, 0:8], cval[:, r, :], LOW)
                    dve.max_index(fpos[:, r, 0:8], fval[:, r, 0:8], cval[:, r, :])
                dve.drain()
                for r in hh:
                    dve.max(fval[:, r, 8:16], cval2[:, r, :])
                dve.drain()
                for r in hh:
                    dve.max_index(fpos[:, r, 8:16], fval[:, r, 8:16], cval2[:, r, :])
                tt(shift[:], fval[:], fval[:, :, 0:1].broadcast_to([P, HEADS, TOPK]),
                   ALU.subtract).then_inc(shifted, 1)
                dve.drain()
                dve.tensor_copy(fposf[:], fpos[:])
                dve.drain()
                yield
                for q in range(HEADS // LOOKUP):
                    hs = slice(LOOKUP * q, LOOKUP * q + LOOKUP)
                    full = [P, LOOKUP, TOPK, NCAND]
                    lk = look[:, :].rearrange("p (a k c) -> p a k c", a=LOOKUP, k=TOPK)
                    lk2 = look[:, :].rearrange("p (r c) -> p r c", c=NCAND)
                    two = [P, LOOKUP * TOPK, NCAND]
                    tt(lk2, bc(fposf[:, hs, :].rearrange("p a k -> p (a k)"), two, 2), bc(cand_no[:], two, 1),
                       ALU.is_equal)
                    dve.drain()
                    tt(lk, lk, bc(cid[:, hs, :], full, 2), ALU.mult)
                    dve.drain()
                    dve.tensor_reduce(fposf[:, hs, :].rearrange("p a k -> p (a k)"), lk2, AX.X, ALU.add)
                    dve.drain()
                    yield
                dve.tensor_copy(ids_ring[:, ring, :], fposf[:, :, :].rearrange("p a k -> p (a k)")).then_inc(ids_ready, 1)
                dve.wait_ge(exped, t + 1)
                seq(lambda: dve.tensor_reduce(fsum[:], shift[:], AX.X, ALU.add),
                    lambda: dve.reciprocal(fsum[:], fsum[:]),
                    lambda: tt(w_ring[:, ring, :].rearrange("p (a k) -> p a k", k=TOPK), shift[:],
                               bc(fsum[:], [P, HEADS, TOPK], 2), ALU.mult))
                dve.drain()
                yield

            def attend(b, i, free):
                t = b * TPB + i
                g = t * HEADS

                def row_max(u):
                    dve.wait_ge(a_s, g + u + 1)
                    dve.tensor_reduce(negmax[:, u % 2:u % 2 + 1], bank[4 + u % 2][:, 0:P * (i + 1)], AX.X, ALU.max,
                                      negate=True).then_inc(a_max, 1)

                def normalise(u):
                    dve.wait_ge(a_o, g + u + 1)
                    dve.reciprocal(rrow[:], psum_row[:, u % 4:u % 4 + 1])
                    dve.drain()
                    ts(o_now[:, D * u:D * u + D], bank[7][:, 0:D], rrow[:, 0:1], None, ALU.mult).then_inc(a_norm, 1)
                    dve.drain()

                yield
                row_max(0)
                yield
                for u in range(HEADS):
                    if u >= 2:
                        normalise(u - 2)
                    if u + 1 < HEADS:
                        row_max(u + 1)
                    yield
                normalise(HEADS - 2)
                normalise(HEADS - 1)
                yield
                yield
                dve.wait_ge(ao_ps, t + 1)
                hi = h[:, t, :]
                tt(hi, hi, bank[7][:, 0:D], ALU.add).then_inc(ao_h, 1)
                dve.drain()
                yield

            def gates(b):
                tile4 = bass.ds(b * TPB, TPB)
                centre(NM, h[:, tile4, :], m_var)
                yield
                scaled(NM, m_rstd, b).then_inc(m_x, 1)
                yield from idle(3)
                dve.wait_ge(xz_sb, 4 * b + 4)
                ts(xmean[:], xsum[:], 1.0 / S, None, ALU.mult).then_inc(mean_in, 1)
                yield
                dve.wait_ge(gsh_ps, b + 1)
                seq(lambda: tt(gsh[:], bank[5][:, 0:4], bg_m[:], ALU.add),
                    lambda: ts(ngsh[:], gsh[:], -1.0, None, ALU.mult).then_inc(gsh_in, 1))
                yield
                dve.wait_ge(sig_e, b + 1)
                g2 = gate[:, :, :].rearrange("p c s -> p (c s)")
                seq(lambda: ts(g2, g2, 1.0, None, ALU.add),
                    lambda: dve.reciprocal(g2, g2))
                dve.drain()
                yield
                for c in (0, 2, 1, 3):
                    last = stt(out=xz[:, c, :], in0=xz[:, c, :], scalar=gsh[:, c:c + 1], in1=gate[:, c, :],
                               op0=ALU.add, op1=ALU.mult)
                last.then_inc(act_in, 1)
                dve.drain()
                yield

            def direction(b, d, tiles):
                m = b * 2 + d
                n0 = m * NST
                xa, zs = xz[:, 2 * d, :], xz[:, 2 * d + 1, :]
                yield
                dve.wait_ge(xd_sb, m + 1)
                seq(lambda: tt(bc_rest[D:P, :], bank[6][D:P, :], bc3[D:P, :], ALU.subtract),
                    lambda: dve.tensor_copy(bc3[D:P, :], bc_rest[D:P, :]),
                    lambda: tt(bc3[96:P, :], bc_rest[96:P, :], bc3[96:P, :], ALU.subtract).then_inc(bc_in, 1))
                dve.drain()
                yield
                dve.wait_ge(sp_e, m + 1)
                seq(lambda: ts(sp_w, sp_u, 2.0, None, ALU.add),
                    lambda: dve.reciprocal(sp_w, sp_w),
                    lambda: tt(sp_u, sp_u, sp_w, ALU.mult),
                    lambda: tt(sp_w, sp_u, sp_u, ALU.mult),
                    lambda: ts(sp_l, sp_w, ATANH[-1], None, ALU.mult))
                dve.drain()
                yield
                seq(*(lambda c=c: stt(out=sp_l, in0=sp_l, scalar=c, in1=sp_w, op0=ALU.add, op1=ALU.mult)
                      for c in ATANH[-2:0:-1]),
                    lambda: stt(out=sp_l, in0=sp_l, scalar=ATANH[0], in1=sp_u, op0=ALU.add, op1=ALU.mult),
                    lambda: tt(dt[:], sp_l, sp_relu, ALU.add).then_inc(dt_in, 1),
                    lambda: tt(dtu[:], dt[:], xa, ALU.mult))
                dve.drain()
                yield
                way = slice(None) if d == 0 else slice(None, None, -1)
                for n in range(NST):
                    dve.wait_ge(B_ps, n0 + n + 1)
                    tt(dBu, dtu[:], bank[4 + 2 * (n % 2)][:, :], ALU.mult).then_inc(dBu_in, 1)
                    dve.drain()
                    dve.wait_ge(dA_in, n0 + n + 1)
                    dve.tensor_tensor_scan(hst[:, way], dA[:, n % 2, way], dBu[:, way], 0.0, ALU.mult,
                                           ALU.add).then_inc(scanned, 1)
                    dve.drain()
                    dve.wait_ge(C_ps, n0 + n + 1)
                    if n >= 2:
                        dve.wait_ge(y_ps, n0 + n - 1)
                    tt(hC[:, n % 2, :], hst, bank[5][:, :], ALU.mult).then_inc(hC_in, 1)
                    yield
                yield
                dve.wait_ge(y_ps, n0 + NST)
                seq(lambda: stt(out=xa, in0=xa, scalar=Dskip[:, d:d + 1], in1=bank[7][:, :], op0=ALU.mult,
                                op1=ALU.add),
                    lambda: tt(gate[:, 2 * d, :], xa, zs, ALU.mult).then_inc(y_in, 1))
                dve.drain()
                yield

            def mix_out(b):
                tile4 = bass.ds(b * TPB, TPB)
                yield
                dve.wait_ge(m_out_ps, b + 1)
                tt(h[:, tile4, :], h[:, tile4, :], bank[6][:, 0:TPB * D].rearrange("p (j d) -> p j d", d=D),
                   ALU.add).then_inc(m_done, 1)
                dve.drain()
                yield

            def experts(b):
                tile4 = bass.ds(b * TPB, TPB)
                centre(NM, h[:, tile4, :], e_var)
                yield
                scaled(NM, e_rstd, b).then_inc(e_x, 1)
                yield from idle(2)
                dve.wait_ge(lg_ps, b + 1)
                four = [P, TPB, EXP]
                tt(lg[:], bank[5][:, 0:TPB * EXP].rearrange("p (j e) -> p j e", e=EXP), bc(ebias[:, 0, :], four, 1),
                   ALU.add).then_inc(lg_read, 1)
                dve.drain()
                tt(lg[:], lg[:], bc(ebias[:, 1, :], four, 1), ALU.add)
                dve.drain()
                yield
                for j in range(TPB):
                    dve.max(lmax[:, j, :], lg[:, j, :])
                dve.drain()
                for j in range(TPB):
                    dve.max_index(lidx[:, j, :], lmax[:, j, :], lg[:, j, :])
                tt(tw[:, 0, :].unsqueeze(2), lmax[:, :, 1:2], lmax[:, :, 0:1], ALU.subtract).then_inc(top_d, 1)
                dve.drain()
                dve.tensor_copy(lidf[:], lidx[:])
                yield
                dve.wait_ge(top_e, b + 1)
                seq(lambda: ts(tw[:, 2, :], tw[:, 1, :], 1.0, None, ALU.add),
                    lambda: dve.reciprocal(tw[:, 2, :], tw[:, 2, :]),
                    lambda: tt(tw[:, 3, :], tw[:, 1, :], tw[:, 2, :], ALU.mult))
                dve.drain()
                for i in range(2):
                    tt(comb[:, i, :, :], bc(exp_no[:], four, 1), lidf[:, :, i:i + 1].broadcast_to(four), ALU.is_equal)
                dve.drain()
                yield
                for i in range(2):
                    tt(comb[:, i, :, :], comb[:, i, :, :], bc(tw[:, 2 + i, :], four, 2), ALU.mult)
                dve.drain()
                tt(comb[:, 0, :, :], comb[:, 0, :, :], comb[:, 1, :, :], ALU.add)
                dve.drain()
                yield
                yield
                for j in range(TPB):
                    dve.wait_ge(y2_ps, TPB * b + j + 1)
                    mixv = gate[:, j, :].rearrange("p (e d) -> p e d", d=D)
                    tt(mixv, bank[4 + j % 2][:, :].rearrange("p (e d) -> p e d", d=D),
                       bc(comb[:, 0, j, :], [P, EXP, D], 2), ALU.mult).then_inc(y2_read, 1)
                    dve.drain()
                    dve.tensor_reduce(ymix[:, j, :], gate[:, j, :].rearrange("p (e d) -> p d e", d=D), AX.X, ALU.add)
                    if j + 1 < TPB:
                        yield
                dve.drain()
                dve.wait_ge(stored, 16 * b)
                tt(hout[:], h[:, tile4, :], ymix[:], ALU.add).then_inc(e_done, 1)
                dve.drain()
                yield

            schedule(dve, (turn_kT, weigh, add_up), route_norm, route, attend, gates, direction, mix_out, experts)


def kernel(**inputs):
    import numpy as np
    import concourse.bacc as bacc
    from concourse.bass_utils import run_bass_kernel_spmd

    a = {k: np.asarray(v) for k, v in inputs.items()}
    f = np.float32
    arrays = {n: a[n] for n in (
        "x", "itok_BS_0_23", "itok_BS_0_11", "itok_BS_0_30", "L0_tok_W1", "L0_tok_b1", "L0_tok_W2", "L0_tok_b2",
        "L0_tok_gamma", "L0_tok_beta", "L0_tok_Wres", "L0_tok_bres", "L0_ffn_Wq_pk", "L0_ffn_Wq", "L0_ffn_Wo",
        "L1_attn_b_dt_f", "L1_attn_b_dt_b", "L1_attn_A_log_f", "L1_attn_A_log_b", "L1_attn_D_f", "L1_attn_D_b",
        "L1_ffn_Wg", "L1_ffn_bg", "L1_ffn_bias", "L1_ffn_W1", "L1_ffn_W2", "L1_ffn_b2")}
    arrays["feature_constants"] = np.array(
        [[1.0 / p, k, c] for p in (7.0, 24.0, 12.0, 1.0) for k in range(1, HARM + 1) for c in (0.0, TWO_PI / 4)], f)
    arrays["hw_by_feature"] = np.repeat(a["L0_tok_hw"].reshape(-1), 2).reshape(FD, 1)
    arrays["ph_by_feature"] = np.repeat(a["L0_tok_ph"].reshape(-1), 2).reshape(FD, 1)
    arrays["keysT"] = a["L0_ffn_pk_keys"].transpose(0, 2, 3, 1).reshape(ROWS, KDIM, NKEY)
    arrays["kv_table"] = np.concatenate([a["L0_ffn_keys_table"], a["L0_ffn_values_table"]], axis=1)
    arrays["W_inT"] = a["L1_attn_W_in"].T
    arrays["W_gT"] = a["L1_attn_W_g"].T
    arrays["b_gT"] = a["L1_attn_b_g"].reshape(4, DI).T
    for s in "fb":
        arrays["W_xpT_" + s] = a["L1_attn_W_xp_" + s].T
        arrays["W_dtT_" + s] = a["L1_attn_W_dt_" + s].T
    arrays["W_outT"] = a["L1_attn_W_out"].T
    arrays["eb1T"] = a["L1_ffn_b1"].T
    arrays = {k: np.ascontiguousarray(v) for k, v in arrays.items()}

    nc = bacc.Bacc("TRN2", target_bir_lowering=False, num_devices=1)
    A = {k: nc.dram_tensor("in_" + k, v.shape, mybir.dt.from_np(v.dtype), kind="ExternalInput").ap()
         for k, v in arrays.items()}
    out = nc.dram_tensor("out", (B, S, D), F32, kind="ExternalOutput").ap()
    program(nc, A, out)
    r = run_bass_kernel_spmd(nc, [{"in_" + k: v for k, v in arrays.items()}], core_ids=[0])
    return r.results[0]["out"]
```

```python
from contextlib import ExitStack

import concourse.bass as bass
from concourse import mybir

ALU = mybir.AluOpType
ACT = mybir.ActivationFunctionType
AX = mybir.AxisListType
F32 = mybir.dt.float32
BF16 = mybir.dt.bfloat16
I32 = mybir.dt.int32
U32 = mybir.dt.uint32

P = 128
D = 64
B, S = 8, 512
TILES = B * S // P
TPB = S // P
EPS = 1e-5

HARM, NPER = 3, 4
FD = NPER * 2 * HARM
GROUPS = 4
GTOK = B * S // GROUPS
TWO_PI = 6.283185307179586
ROUND = 12582912.0
PI_A, PI_B, PI_C = 6.28125, 0.0019350051879882812, 3.019916050561733e-07
PI_MAX = 3.1415925

HEADS = 8
NKEY = 64
TOPK = 16
KDIM = 32
ROWS = 2 * HEADS
CAND = [TOPK // (a + 1) for a in range(TOPK)]
NCAND = sum(CAND)
WIDE = sum(1 for n in CAND if n > 1)
LOW = -3.0e38
SLOTS = 4
RING = 8
XRING = 4
FOLD = TOPK // 4
LOOKUP = 2

PARTS = [(0, 1), (1, TPB)] + [(TPB * q, TPB * q + TPB) for q in range(1, B)]
PARTS_BEFORE = [5, 7, B + 1]

DI, NST, RANK = 128, 16, 16
ATANH = (2.0, 0.6666632294654846, 0.4002459645271301, 0.27965158224105835, 0.28157779574394226)

EXP, EDIM = 8, 128

PART_STEPS = TILES // 2 + 4
ROUTE_STEPS, NORM_STEPS = 12, 3
ATTEND_STEPS = HEADS + 5
GATES_STEPS, OUT_STEPS, EXPERTS_STEPS = 8, 2, 12
DIRECTION_STEPS = NST + 6
PART_AFTER = 6
AHEAD = 2


def program(nc, A, out):
    ctx = ExitStack()
    with ctx:
        def sb(name, shape, dt=F32):
            return ctx.enter_context(nc.sbuf_tensor(name, shape, dt))

        def sem(name):
            return ctx.enter_context(nc.semaphore(name))

        bank = [ctx.enter_context(nc.psum_tensor(f"bank{i}", [P, 512], F32)) for i in range(8)]

        h = sb("h", [P, TILES, D])
        xT = sb("xT", [D, XRING * S])
        idf = sb("idf", [P, P])
        idb = sb("idb", [P, P], BF16)
        causal = sb("causal", [P, P], BF16)
        cand_no = sb("cand_no", [P, NCAND])
        head_base = sb("head_base", [P, HEADS, TOPK])
        exp_no = sb("exp_no", [P, EXP])
        ones = sb("ones", [1, P])
        spread3 = sb("spread3", [P, 2 * NST], BF16)

        w_feat = sb("w_feat", [P, 5 + 128 + D])
        tW1, tWres = w_feat[:, 5:5 + 128], w_feat[:, 5 + 128:]
        tW2 = sb("tW2", [128, D])
        tb1 = sb("tb1", [P, 1])
        trow = sb("trow", [P, 4, D])
        wqpk = sb("wqpk", [D, ROWS * KDIM])
        keys = sb("keys", [P, 4, 4 * NKEY])
        wq = sb("wq", [D, HEADS * D])
        wo = sb("wo", [P, 4, D])
        winT = sb("winT", [D, 4 * DI])
        wgT = sb("wgT", [P, 4, 4 * DI])
        bg_m = sb("bg_m", [P, 4])
        wxpT = sb("wxpT", [P, 2, P])
        wdtT = sb("wdtT", [RANK, 2, DI])
        bdt = sb("bdt", [P, 2])
        negA = sb("negA", [P, 2, NST])
        Dskip = sb("Dskip", [P, 2])
        woutT = sb("woutT", [P, 2, D])
        eWg = sb("eWg", [D, EXP])
        ebias = sb("ebias", [P, 2, EXP])
        eW1 = sb("eW1", [D, EXP, EDIM])
        eb1 = sb("eb1", [P, EXP])
        eW2 = sb("eW2", [P, EXP, D])
        eb2 = sb("eb2", [1, EXP * D])

        rows = sb("rows", [P, SLOTS, TOPK, 2 * D])
        ids_ring = sb("ids_ring", [P, RING, HEADS * TOPK], U32)
        ids_now = sb("ids_now", [P, 2, HEADS * TOPK], U32)
        w_ring = sb("w_ring", [P, RING, HEADS * TOPK])
        qpkT = sb("qpkT", [P, 4, P])
        sim = sb("sim", [P, ROWS, NKEY])
        best = sb("best", [P, ROWS, TOPK])
        besti = sb("besti", [P, ROWS, TOPK], U32)
        bestf = sb("bestf", [P, ROWS, TOPK])
        cval = sb("cval", [P, HEADS, NCAND])
        cid = sb("cid", [P, HEADS, NCAND])
        fval = sb("fval", [P, HEADS, TOPK])
        fpos = sb("fpos", [P, HEADS, TOPK], U32)
        fposf = sb("fposf", [P, HEADS, TOPK])
        look = sb("look", [P, LOOKUP * TOPK * NCAND])
        assert LOOKUP * TOPK * NCAND >= ROWS * NKEY
        sim2 = look[:, 0:ROWS * NKEY].rearrange("p (r k) -> p r k", r=ROWS)
        cval2 = look[:, 0:HEADS * NCAND].rearrange("p (r k) -> p r k", r=HEADS)
        shift = sb("shift", [P, HEADS, TOPK])
        fsum = sb("fsum", [P, HEADS])
        k_now = sb("k_now", [P, HEADS * D])
        kT = sb("kT", [P, 2, 4, S])
        val = sb("val", [P, 2, TPB, HEADS, D])

        prob = sb("prob", [P, 2, S])
        probT = sb("probT", [P, 2, 4, P])
        o_now = sb("o_now", [P, HEADS * D])
        oT = sb("oT", [P, 4, P])
        negmax = sb("negmax", [P, 2])
        psum_row = sb("psum_row", [P, 4])
        qz = sb("qz", [P, HEADS, P])
        rrow = sb("rrow", [P, 1])

        xzg = sb("xzg", [P, 8, S])
        xz, gate = xzg[:, 0:4, :], xzg[:, 4:8, :]
        xsum = sb("xsum", [P, 4])
        xmean = sb("xmean", [P, 4])
        gsh = sb("gsh", [P, 4])
        ngsh = sb("ngsh", [P, 4])
        bc3 = sb("bc3", [P, S], BF16)
        dt = sb("dt", [P, S])
        dtu = sb("dtu", [P, S])
        mwork = sb("mwork", [P, 8, S])
        dA = mwork[:, 0:2, :]
        hC = mwork[:, 2:4, :]
        dBu = mwork[:, 4, :]
        hst = mwork[:, 5, :]
        bc_rest = mwork[:, 6, :]
        dt_low = mwork[0:RANK, 7, :]
        sp_relu, sp_u, sp_w, sp_l = (mwork[:, i, :] for i in (0, 1, 2, 3))
        hid = mwork

        def norm_set(tag):
            return dict(
                xc=sb(f"xc_{tag}", [P, TPB, D]), sq=sb(f"sq_{tag}", [P, TPB, D]),
                s=sb(f"s_{tag}", [P, TPB]), v=sb(f"v_{tag}", [P, TPB]), y0=sb(f"y0_{tag}", [P, TPB]),
                t=sb(f"t_{tag}", [P, TPB]), r=sb(f"r_{tag}", [P, TPB]), l=sb(f"l_{tag}", [P, TPB]))
        NR, NM = norm_set("r"), norm_set("m")
        xt4 = dtu[0:D, :]
        lg = sb("lg", [P, TPB, EXP])
        lmax = sb("lmax", [P, TPB, 8])
        lidx = sb("lidx", [P, TPB, 8], U32)
        lidf = sb("lidf", [P, TPB, 8])
        tw = sb("tw", [P, 4, TPB])
        comb = sb("comb", [P, 2, TPB, EXP])
        ymix = sb("ymix", [P, TPB, D])
        hout = sb("hout", [P, TPB, D])

        half = [P, TILES // 2, D]
        f1 = xzg[:, :, :].rearrange("p c s -> p (c s)")[:, 0:TILES * (D + 1)].rearrange("p (t d) -> p t d", d=D + 1)
        F1 = -(-TILES * (D + 1) // S)
        esc = xzg[:, F1:F1 + 2, :]
        fT = mwork[0:D, :, :].rearrange("p c s -> p (c s)")
        uT = dtu[0:D + 1, :]
        stats = val[:, 0, :, :, :].rearrange("p j a d -> p (j a d)")
        NE = []
        for i in range(2):
            NE.append({x: stats[:, 16 * (7 * i + k):16 * (7 * i + k) + 16] for k, x in
                       enumerate(("s", "v", "y0", "t", "r", "l", "r1"))})
            for k, x in enumerate(("xc", "sq")):
                NE[i][x] = kT[:, k, :, :].rearrange("p c s -> p (c s)").rearrange("p (t d) -> p t d", d=D)[
                    :, TILES // 2 * i:TILES // 2 * (i + 1), :]
        feat = xz[:, 0:2, :].rearrange("p a s -> p (a s)")
        idsb = xz[:, 2:4, :].rearrange("p a s -> p (a s)").bitcast(I32)
        ang = gate[:, 0:2, :].rearrange("p a s -> p (a s)")
        turn = gate[:, 2:4, :].rearrange("p a s -> p (a s)")
        h1 = mwork[:, 1:3, :]

        loaded = sem("loaded")
        ids_in, w_feat_in = sem("ids_in"), sem("w_feat_in")
        consts = sem("consts")
        weights_zeroed = sem("weights_zeroed")
        angle_done, feat_done, scaled_feat = sem("angle_done"), sem("feat_done"), sem("scaled_feat")
        h1_ps, h1_sb, h2_ps, h2_read = sem("h1_ps"), sem("h1_sb"), sem("h2_ps"), sem("h2_read")
        t_var, t_rstd = sem("t_var"), sem("t_rstd")
        u_var, u_rstd, u_sq, u_rl2 = sem("u_var"), sem("u_rstd"), sem("u_sq"), sem("u_rl2")
        f_done, fT_ps, fT_sb = sem("f_done"), sem("fT_ps"), sem("fT_sb")
        mixed = sem("mixed")
        score_ps, score_exp, mix_sb = sem("score_ps"), sem("score_exp"), sem("mix_sb")
        mixT_ps, mixT_read, m_sq, m_rl2 = sem("mixT_ps"), sem("mixT_read"), sem("m_sq"), sem("m_rl2")
        r_var, r_rstd, r_x, r_xT_ps, r_xT = (sem("r_" + x) for x in ("var", "rstd", "x", "xT_ps", "xT"))
        q_ps, q_sb, sim_ps, sim_sb = sem("q_ps"), sem("q_sb"), sem("sim_ps"), sem("sim_sb")
        picked, shifted, exped, ids_ready = sem("picked"), sem("shifted"), sem("exped"), sem("ids_ready")
        landed = [sem(f"landed{i}") for i in range(SLOTS)]
        routed = sem("routed")
        weighted, summed, kv_sb, kT_ps, kT_sb = (sem(x) for x in ("weighted", "summed", "kv_sb", "kT_ps", "kT_sb"))
        aq_ps, aq_sb = sem("aq_ps"), sem("aq_sb")
        a_s, a_max, a_exp, a_T, a_Tsb, a_o, a_norm = (sem("a_" + x) for x in ("s", "max", "exp", "T", "Tsb", "o", "norm"))
        ao_T, ao_sb, ao_ps, ao_h = sem("ao_T"), sem("ao_sb"), sem("ao_ps"), sem("ao_h")
        m_var, m_rstd, m_x, m_xT_ps, m_xT = (sem("m_" + x) for x in ("var", "rstd", "x", "xT_ps", "xT"))
        xz_ps, xz_sb, mean_in, gsh_ps, gsh_in, sig_e, act_in = (
            sem(x) for x in ("xz_ps", "xz_sb", "mean_in", "gsh_ps", "gsh_in", "sig_e", "act_in"))
        xd_ps, xd_sb, dt_ps, sp_e, dt_in = (sem(x) for x in ("xd_ps", "xd_sb", "dt_ps", "sp_e", "dt_in"))
        bc_in = sem("bc_in")
        B_ps, C_ps, dA_in, dBu_in, scanned, hC_in, y_ps = (
            sem(x) for x in ("B_ps", "C_ps", "dA_in", "dBu_in", "scanned", "hC_in", "y_ps"))
        y_in, m_out_ps, m_done = sem("y_in"), sem("m_out_ps"), sem("m_done")
        e_var, e_rstd, e_x, e_xT_ps, e_xT = (sem("e_" + x) for x in ("var", "rstd", "x", "xT_ps", "xT"))
        lg_ps, lg_read, top_d, top_e, hid_ps, hid_sb, y2_ps, y2_read, e_done = (
            sem(x) for x in ("lg_ps", "lg_read", "top_d", "top_e", "hid_ps", "hid_sb", "y2_ps", "y2_read", "e_done"))
        stored = sem("stored")

        block = ctx.enter_context(nc.Block())

        def count(n):
            return max(n, 0) if isinstance(n, int) else n

        def t_is(b, j, t):
            return isinstance(b, int) and isinstance(j, int) and b * TPB + j == t

        def norms(b, hi):
            return 0 if hi == 1 else b + 1

        def folds(b):
            return isinstance(b, int) and b == 0

        def few(N, tiles):
            return {x: N[x][:, 0:tiles] if len(N[x].shape) == 2 else N[x][:, 0:tiles, :] for x in N}

        def idle(steps):
            for _ in range(steps):
                yield

        def schedule(eng, all_tokens, hand_over, sums, route_norm, route, attend, gates, direction, mix_out, experts):
            weigh, add_up, turn_kT = sums

            def routing(b, tiles, more=True):
                if t_is(b, 0, 0):
                    yield from route_norm(0, 1, TPB)
                for j in tiles:
                    yield from route(b * TPB + j)
                if more:
                    yield from route_norm(b + 1)
                    for j in range(AHEAD):
                        yield from route((b + 1) * TPB + j)

            def mamba_experts(b):
                yield from gates(b)
                for d in range(2):
                    yield from direction(b, d, (b + 1) * TPB)
                yield from mix_out(b)
                yield from experts(b)

            def tower(b):
                yield from attend(b - 1, TPB - 1, (ao_h, b * TPB - 1))
                yield from gates(b - 1)
                yield from direction(b - 1, 0, b * TPB)
                yield from attend(b, 0, (y_in, 2 * b - 1))
                yield from direction(b - 1, 1, b * TPB + 1)
                yield from mix_out(b - 1)
                yield from attend(b, 1, (m_done, b))
                yield from experts(b - 1)
                yield from attend(b, 2, (y2_read, b * TPB))

            def first_tower():
                q = 2
                for i, end in enumerate(PARTS_BEFORE):
                    while q < end:
                        yield from all_tokens(q, (ao_h, i))
                        q += 1
                    yield from attend(0, i, (mixT_read, q))

            def evenly(steps, units=TPB * HEADS):
                return [steps * (u + 1) // units - steps * u // units for u in range(units)]

            def paced(stages, units=TPB * HEADS):
                weights = [w for steps, w in stages for _ in range(steps)]
                at, found = 0, [0] * units
                for w in weights:
                    found[int(at * units / sum(weights))] += 1
                    at += w
                return found

            def weave(lines, u):
                for line, steps in lines:
                    for _ in range(steps[u]):
                        next(line)

            def batch(b, *lines):
                for u in range(TPB * HEADS):
                    j, hd = divmod(u, HEADS)
                    if u == 0 and not t_is(b, j, 0):
                        turn_kT(b - 1, TPB - 1, 3)
                    elif u > 0 and u % 2 == 0:
                        turn_kT(*((b, j, hd // 2 - 1) if hd > 0 else (b, j - 1, 3)))
                    weigh(b, j, hd)
                    weave(lines, u)
                    add_up(b, j, hd)

            def many(*stages):
                for stage in stages:
                    yield from stage

            for _ in all_tokens(0, (consts, 1)):
                pass
            beside = all_tokens(1, (consts, 1))
            lines = [(beside, evenly(PART_STEPS - PART_AFTER, ROUTE_STEPS + NORM_STEPS)),
                     (many(route_norm(0, 0, 1), route(0)), evenly(ROUTE_STEPS + NORM_STEPS, ROUTE_STEPS + NORM_STEPS))]
            for u in range(ROUTE_STEPS + NORM_STEPS):
                weave(lines, u)
            hand_over(0, 0)
            for _ in beside:
                pass
            weights = []
            for i, (q, end) in enumerate(zip([2] + PARTS_BEFORE, PARTS_BEFORE)):
                weights += [((end - q) * PART_STEPS, 6), (ATTEND_STEPS, 3 + i)]
            batch(0, (first_tower(), paced(weights)),
                  (routing(0, range(1, TPB)), [3] * 5 + [2] * 6 + evenly(3 * ROUTE_STEPS + NORM_STEPS, 21)))
            turn = lambda i: (ATTEND_STEPS, 22 + 6 * i)
            weights = [turn(3), (GATES_STEPS, 34), (DIRECTION_STEPS, 29), turn(0), (DIRECTION_STEPS, 29),
                       (OUT_STEPS, 20), turn(1), (EXPERTS_STEPS, 30), turn(2)]
            with eng.Fori(1, B - 1) as b:
                batch(b, (tower(b), paced(weights)), (routing(b, range(AHEAD, TPB)), evenly(TPB * ROUTE_STEPS + NORM_STEPS)))
            last = attend(B - 1, TPB - 1, (ao_h, B * TPB - 1))
            batch(B - 1, (tower(B - 1), paced(weights[:-1], (TPB - 1) * HEADS) + [5, 5, ATTEND_STEPS - 10] + [0] * 5),
                  (routing(B - 1, range(AHEAD, TPB), more=False),
                   evenly((TPB - AHEAD) * ROUTE_STEPS, 18) + [0] * 14),
                  (last, [0] * (TPB - 1) * HEADS + [0, 0, 0, 3, 2, 0, 2, 0]))
            turn_kT(B - 1, TPB - 1, 3)
            for _ in many(last, mamba_experts(B - 1)):
                pass

        settled = {}

        def settle(eng):
            if eng not in settled:
                settled[eng] = sem(f"settled{len(settled)}")
            eng.sem_inc(settled[eng], 1)

        def bc(ap, shape, axis):
            return ap.unsqueeze(axis).broadcast_to(shape)

        n_loads = []

        @block.sync
        def _(sp):

            def load(dst, src):
                sp.dma_start(dst, src).then_inc(loaded, 16)
                n_loads.append(1)

            sp.sem_inc(stored, 16)
            sp.dma_start(idsb, A["ids_by_feature"]).then_inc(ids_in, 16)
            sp.dma_start(w_feat[:], A["feature_weights"]).then_inc(w_feat_in, 16)
            load(tW2[:], A["L0_tok_W2"])
            load(tb1[:], A["L0_tok_b1"].unsqueeze(1))
            for i, name in enumerate(("L0_tok_b2", "L0_tok_gamma", "L0_tok_beta", "L0_tok_bres")):
                load(trow[:, i, :], bc(A[name], [P, D], 0))
            load(wqpk[:], A["L0_ffn_Wq_pk"])
            load(wq[:], A["L0_ffn_Wq"])
            load(wo[:], A["L0_ffn_Wo"].rearrange("(c p) n -> p c n", p=P))
            load(winT[:], A["W_inT"])
            load(wgT[:], A["W_gT"].rearrange("(c p) n -> p c n", p=P))
            load(bg_m[:], A["b_gT"])
            sp.wait_ge(weights_zeroed, 1)
            for d, s in enumerate("fb"):
                load(wxpT[:, d, 0:RANK], A["W_xpT_" + s][:, 0:RANK])
                for i in range(1, 4):
                    load(wxpT[:, d, 2 * NST * i:2 * NST * (i + 1)], A["W_xpT_" + s][:, RANK:RANK + 2 * NST])
                load(wdtT[:, d, :], A["W_dtT_" + s])
                load(bdt[:, d:d + 1], A["L1_attn_b_dt_" + s].unsqueeze(1))
                load(negA[:, d, :], A["L1_attn_A_log_" + s])
                load(Dskip[:, d:d + 1], A["L1_attn_D_" + s].unsqueeze(1))
            load(woutT[:], A["W_outT"].rearrange("(c p) n -> p c n", p=P))
            load(eWg[:], A["L1_ffn_Wg"])
            load(ebias[:, 0, :], bc(A["L1_ffn_bg"], [P, EXP], 0))
            load(ebias[:, 1, :], bc(A["L1_ffn_bias"], [P, EXP], 0))
            load(eW1[:], A["L1_ffn_W1"].rearrange("e d f -> d e f"))
            load(eb1[:], A["eb1T"])
            load(eW2[:], A["L1_ffn_W2"].rearrange("e f d -> f e d"))
            load(eb2[:], A["L1_ffn_b2"].rearrange("e d -> (e d)").unsqueeze(0))
            for g in range(4):
                load(keys[32 * g:32 * g + 32, :, NKEY * g:NKEY * g + NKEY],
                     A["keysT"].rearrange("(c g) d k -> g d c k", g=4)[g])
            out_v = out.rearrange("b s d -> (b s) d").rearrange("(t p) d -> p t d", p=P)
            with sp.Fori(0, B) as b:
                sp.wait_ge(e_done, b + 1)
                sp.dma_start(out_v[:, bass.ds(b * TPB, TPB), :], hout[:]).then_inc(stored, 16)
                sp.wait_ge(stored, 16 * b + 32)
                settle(sp)

        LOADS = len(n_loads)

        @block.gpsimd
        def _(pool):
            pool.memset(idf[:], 0.0)
            pool.memset(idb[:], 0.0)
            pool.memset(causal[:], 0.0)
            pool.memset(ones[:], 1.0)
            pool.memset(wxpT[:], 0.0)
            pool.memset(qz[:], 0.0)
            pool.memset(keys[:], 0.0).then_inc(weights_zeroed, 1)
            pool.drain()
            pool.affine_select(out=idf[:], in_=idf[:], compare_op=ALU.not_equal, fill=1.0, base=0,
                               pattern=[[-1, P]], channel_multiplier=1)
            pool.affine_select(out=idb[:], in_=idb[:], compare_op=ALU.not_equal, fill=1.0, base=0,
                               pattern=[[-1, P]], channel_multiplier=1)
            pool.affine_select(out=causal[:], in_=causal[:], compare_op=ALU.is_ge, fill=-1e30, base=0,
                               pattern=[[-1, P]], channel_multiplier=1)
            pool.iota(cand_no[:], pattern=[[1, NCAND]], base=0, channel_multiplier=0,
                      allow_small_or_imprecise_dtypes=True)
            pool.iota(exp_no[:], pattern=[[1, EXP]], base=0, channel_multiplier=0,
                      allow_small_or_imprecise_dtypes=True)
            pool.iota(head_base[:], pattern=[[NKEY * NKEY, HEADS], [0, TOPK]], base=0, channel_multiplier=0,
                      allow_small_or_imprecise_dtypes=True).then_inc(consts, 1)
            with pool.Fori(0, TILES // 2) as t2:
                for u in range(2):
                    t = t2 * 2 + u
                    pool.wait_ge(ids_ready, t + 1)
                    for hd in range(HEADS):
                        pool.wait_ge(summed, t * HEADS + hd + 1)
                        settle(pool)
                        for k in range(TOPK):
                            c = hd * TOPK + k
                            pool.indirect_dma_start(
                                rows[:, hd % SLOTS, k, :], None, A["kv_table"],
                                bass.IndirectOffsetOnAxis(ap=ids_now[:, u, c:c + 1], axis=0),
                            ).then_inc(landed[hd % SLOTS], 16)

        @block.tensor
        def _(pe):
            mm = pe.matmul
            pe.wait_ge(consts, 1)

            def hidden(n):
                c, g = divmod(n, GROUPS)
                r = slice(32 * g, 32 * g + FD)
                pe.wait_ge(h1_sb, max(n - 1, 0))
                mm(bank[n % 2][:, :], tW1[r, :], feat[r, c * S:c * S + S], start=True, stop=True).then_inc(h1_ps, 1)

            pe.wait_ge(scaled_feat, 1)
            hidden(0)
            pe.wait_ge(loaded, 16 * LOADS)
            for n in range(2 * GROUPS):
                c, g = divmod(n, GROUPS)
                r = slice(32 * g, 32 * g + FD)
                if n + 1 < 2 * GROUPS:
                    hidden(n + 1)
                pe.wait_ge(h1_sb, n + 1)
                pe.wait_ge(h2_read, max(n - 1, 0))
                for j in range(TPB):
                    ps = bank[2 + n % 2]
                    mm(ps[:, D * j:D * j + D], h1[:, n % 2, P * j:P * j + P], tW2[:], start=True, stop=True)
                    last = mm(ps[:, 256 + D * j:256 + D * j + D], feat[r, c * S + P * j:c * S + P * j + P], tWres[r, :],
                              start=True, stop=True)
                last.then_inc(h2_ps, 1)

            for q in range(B):
                pe.wait_ge(f_done, 1 + q // (B // 2))
                pe.wait_ge(fT_sb, max(q - 1, 0))
                for j in range(TPB):
                    last = pe.transpose(bank[q % 2][0:D, P * j:P * j + P], f1[:, q * TPB + j, 0:D], idf[:])
                last.then_inc(fT_ps, 1)

            def all_tokens(q, free):
                n = q * TILES
                lo, hi = PARTS[q]
                w = P * (hi - lo)

                def scores(j):
                    pe.wait_ge(score_exp, max(n + j - 1, 0))
                    mm(bank[4 + j % 2][:, 0:w], fT[:, P * j:P * j + P], fT[:, P * lo:P * hi],
                       start=True, stop=True).then_inc(score_ps, 1)

                pe.wait_ge(free[0], free[1])
                pe.wait_ge(fT_sb, B)
                scores(0)
                yield
                for j in range(TILES):
                    if j + 1 < TILES:
                        scores(j + 1)
                    pe.wait_ge(score_exp, n + j + 1)
                    mm(bank[7][0:D + 1, 0:w], f1[:, j, :], esc[:, j % 2, 0:w], start=(j == 0),
                       stop=(j == TILES - 1)).then_inc(mixed, 1)
                    if j % 2 == 1:
                        yield
                yield
                pe.wait_ge(mix_sb, q + 1)
                pe.wait_ge(mixT_read, q)
                for j in range(hi - lo):
                    last = pe.transpose(bank[6][:, (D + 1) * j:(D + 1) * (j + 1)], uT[:, P * j:P * j + P],
                                        idf[0:D + 1, 0:D + 1])
                last.then_inc(mixT_ps, 1)
                yield
                yield

            def turn_kT(b, j, c):
                p = (b * TPB + j) * 4 + c
                pe.wait_ge(kv_sb, 2 * p + 2)
                pe.transpose(bank[3][:, 0:P], k_now[:, P * c:P * c + P], idf[:]).then_inc(kT_ps, 1)

            def weigh(b, j, hd):
                pass

            def add_up(b, j, hd):
                m = (b * TPB + j) * HEADS + hd
                pe.wait_ge(weighted, m + 1)
                pe.wait_ge(kv_sb, count(m - 1))
                if hd % 2 == 1:
                    pe.wait_ge(kT_sb, count((b * TPB + j) * 4 + hd // 2))
                n = FOLD if folds(b) else TOPK
                for k in range(n):
                    last = mm(bank[3 * (hd % 2)][:, 0:2 * D], idf[:], rows[:, hd % SLOTS, k, :],
                              start=(k == 0), stop=(k == n - 1))
                last.then_inc(summed, 1)

            def route_norm(b, lo=0, hi=TPB):
                yield from idle(2)
                pe.wait_ge(r_x, norms(b, hi) + 1)
                pe.wait_ge(sim_sb, b * TPB + lo)
                settle(pe)
                for j in range(hi - lo):
                    last = pe.transpose(bank[1][0:D, P * j:P * j + P], NR["sq"][:, j, :], idf[:])
                last.then_inc(r_xT_ps, 1)
                yield

            def route(t):
                pe.wait_ge(r_xT, 1 if t_is(0, t, 0) else t // TPB + 2)
                pe.wait_ge(sim_sb, t)
                settle(pe)
                for c in range(4):
                    last = mm(bank[1][:, P * c:P * c + P], wqpk[:, P * c:P * c + P],
                              xT[:, bass.ds((t % (XRING * TPB)) * P, P)], start=True, stop=True)
                last.then_inc(q_ps, 1)
                yield
                pe.wait_ge(q_sb, t + 1)
                for c in range(4):
                    last = mm(bank[1 + c // 2][:, 256 * (c % 2):256 * (c % 2) + 256], qpkT[:, c, :], keys[:, c, :],
                              start=True, stop=True)
                last.then_inc(sim_ps, 1)
                yield from idle(ROUTE_STEPS - 1)

            def attend(b, i, free):
                par = b % 2
                t = b * TPB + i
                g = t * HEADS

                def scores(u):
                    pe.wait_ge(a_exp, count(g + u - 1))
                    if u % 2 == 0:
                        pe.wait_ge(kT_sb, 4 * t + u // 2 + 1)
                    ps = bank[4 + u % 2]
                    mm(ps[:, 0:P * (i + 1)], qz[:, u, :], kT[:, par, u // 2, 0:P * (i + 1)], start=True, stop=False)
                    mm(ps[:, P * i:P * i + P], idb[:], causal[:], start=False, stop=True).then_inc(a_s, 1)

                def turn_probs(u):
                    pe.wait_ge(a_exp, g + u + 1)
                    pe.wait_ge(a_Tsb, g + u)
                    for j in range(i + 1):
                        last = pe.transpose(bank[6][:, P * j:P * j + P], prob[:, u % 2, P * j:P * j + P], idf[:])
                    last.then_inc(a_T, 1)

                def mix_values(u):
                    pe.wait_ge(a_Tsb, g + u + 1)
                    pe.wait_ge(a_norm, g + u)
                    for j in range(i + 1):
                        last = mm(bank[7][:, 0:D], probT[:, u % 2, j, :], val[:, par, j, u, :],
                                  start=(j == 0), stop=(j == i))
                    last.then_inc(a_o, 1)

                pe.wait_ge(free[0], free[1])
                settle(pe)
                for c in range(4):
                    last = mm(bank[6][:, P * c:P * c + P], wq[:, P * c:P * c + P],
                              xT[:, bass.ds((t % (XRING * TPB)) * P, P)], start=True, stop=True)
                last.then_inc(aq_ps, 1)
                yield
                pe.wait_ge(aq_sb, t + 1)
                scores(0)
                yield
                for u in range(HEADS):
                    if u + 1 < HEADS:
                        scores(u + 1)
                    turn_probs(u)
                    if u > 0:
                        mix_values(u - 1)
                    yield
                mix_values(HEADS - 1)
                yield
                pe.wait_ge(a_norm, g + HEADS)
                for c in range(4):
                    last = pe.transpose(bank[6][:, P * c:P * c + P], o_now[:, P * c:P * c + P], idf[:])
                last.then_inc(ao_T, 1)
                yield
                pe.wait_ge(ao_sb, t + 1)
                for c in range(4):
                    last = mm(bank[7][:, 0:D], oT[:, c, :], wo[:, c, :], start=(c == 0), stop=(c == 3))
                last.then_inc(ao_ps, 1)
                yield

            def gates(b):
                yield from idle(2)
                pe.wait_ge(m_x, b + 1)
                settle(pe)
                for j in range(TPB):
                    last = pe.transpose(bank[4][0:D, P * j:P * j + P], NM["sq"][:, j, :], idf[:])
                last.then_inc(m_xT_ps, 1)
                yield
                pe.wait_ge(m_xT, b + 1)
                for c in range(4):
                    mm(bank[4 + (c + 1) % 4][:, :], winT[:, P * c:P * c + P], xt4, start=True,
                       stop=True).then_inc(xz_ps, 1)
                yield
                pe.wait_ge(mean_in, b + 1)
                for m in range(4):
                    for k in range(4):
                        last = mm(bank[5][:, m:m + 1], wgT[:, k, P * m:P * m + P], xmean[:, k:k + 1],
                                  start=(k == 0), stop=(k == 3))
                last.then_inc(gsh_ps, 1)
                yield from idle(GATES_STEPS - 4)

            def direction(b, d, tiles):
                m = b * 2 + d
                n0 = m * NST

                def spread_B(n):
                    if n >= 2:
                        pe.wait_ge(dBu_in, n0 + n - 1)
                    mm(bank[4 + 2 * (n % 2)][:, :], spread3[:, n:n + 1].broadcast_to([P, P]), bc3[:],
                       start=True, stop=True).then_inc(B_ps, 1)

                def spread_C(n):
                    if n >= 1:
                        pe.wait_ge(hC_in, n0 + n)
                    mm(bank[5][:, :], spread3[:, NST + n:NST + n + 1].broadcast_to([P, P]), bc3[:],
                       start=True, stop=True).then_inc(C_ps, 1)

                def add_y(n):
                    pe.wait_ge(hC_in, n0 + n + 1)
                    mm(bank[7][:, :], idf[:], hC[:, n % 2, :], start=(n == 0), stop=(n == NST - 1)).then_inc(y_ps, 1)

                pe.wait_ge(act_in, b + 1)
                mm(bank[6][:, :], wxpT[:, d, :], xz[:, 2 * d, :], start=True, stop=True).then_inc(xd_ps, 1)
                yield
                pe.wait_ge(ao_h, tiles)
                if d == 1:
                    pe.wait_ge(y_in, m)
                pe.wait_ge(xd_sb, m + 1)
                mm(bank[7][:, :], wdtT[:, d, :], dt_low, start=True, stop=True).then_inc(dt_ps, 1)
                yield
                yield
                pe.wait_ge(bc_in, m + 1)
                spread_B(0)
                pe.wait_ge(sp_e, m + 1)
                yield
                for n in range(NST):
                    spread_C(n)
                    if n + 1 < NST:
                        spread_B(n + 1)
                    if n > 0:
                        add_y(n - 1)
                    yield
                add_y(NST - 1)
                yield from idle(2)

            def mix_out(b):
                pe.wait_ge(y_in, 2 * b + 2)
                for j in range(TPB):
                    for d in range(2):
                        last = mm(bank[6][:, D * j:D * j + D], gate[:, 2 * d, P * j:P * j + P], woutT[:, d, :],
                                  start=(d == 0), stop=(d == 1))
                last.then_inc(m_out_ps, 1)
                yield from idle(OUT_STEPS)

            def experts(b):
                yield from idle(2)
                pe.wait_ge(e_x, b + 1)
                settle(pe)
                for j in range(TPB):
                    last = pe.transpose(bank[4][0:D, P * j:P * j + P], NM["sq"][:, j, :], idf[:])
                last.then_inc(e_xT_ps, 1)
                yield
                pe.wait_ge(e_xT, b + 1)
                for j in range(TPB):
                    last = mm(bank[5][:, EXP * j:EXP * j + EXP], xt4[:, P * j:P * j + P], eWg[:], start=True, stop=True)
                last.then_inc(lg_ps, 1)
                for e in range(EXP):
                    if e >= 2:
                        pe.wait_ge(hid_sb, EXP * b + e - 1)
                    mm(bank[6 + e % 2][:, :], eW1[:, e, :], xt4, start=True, stop=True).then_inc(hid_ps, 1)
                    if e % 2 == 1:
                        yield
                pe.wait_ge(lg_read, b + 1)
                pe.wait_ge(hid_sb, EXP * b + EXP)
                for j in range(TPB):
                    ps = bank[4 + j % 2]
                    if j >= 2:
                        pe.wait_ge(y2_read, TPB * b + j - 1)
                    mm(ps[:, :], ones[:], eb2[:], start=True, stop=False)
                    for e in range(EXP):
                        last = mm(ps[:, D * e:D * e + D], hid[:, e, P * j:P * j + P], eW2[:, e, :],
                                  start=False, stop=(e == EXP - 1))
                    last.then_inc(y2_ps, 1)
                    yield
                yield

            schedule(pe, all_tokens, lambda t, parity: None, (weigh, add_up, turn_kT), route_norm, route, attend, gates, direction, mix_out, experts)

        @block.scalar
        def _(act):
            ac = act.activation
            act.wait_ge(consts, 1)

            def rstd(N, done_v, done_r, n, scale=1.0):
                act.wait_ge(done_v, n + 1)
                ac(N["l"][:], N["v"][:], ACT.Ln, scale=scale)
                act.drain()
                ac(N["y0"][:], N["l"][:], ACT.Exp, scale=-0.5).then_inc(done_r, 1)

            act.wait_ge(angle_done, 1)
            ac(feat, ang, ACT.Sin).then_inc(feat_done, 1)
            act.preload_act_table_set("natural_log_exp_and_others")
            act.wait_ge(loaded, 16 * LOADS)
            ac(negA[:], negA[:], ACT.Exp)
            act.drain()
            ac(negA[:], negA[:], ACT.Copy, scale=-1.0)

            def relu(n):
                act.wait_ge(h1_ps, n + 1)
                act.wait_ge(h2_ps, max(n - 1, 0))
                ac(h1[:, n % 2, :], bank[n % 2][:, :], ACT.Relu, bias=tb1[:, 0:1]).then_inc(h1_sb, 1)

            for n in range(5):
                relu(n)
            rstd(NE[0], t_var, t_rstd, 0)
            relu(5)
            relu(6)
            rstd(NE[0], u_var, u_rstd, 0)
            relu(7)
            rstd(NE[0], u_sq, u_rl2, 0, scale=2.0 ** 40)
            rstd(NE[1], t_var, t_rstd, 1)
            rstd(NE[1], u_var, u_rstd, 1)
            rstd(NE[1], u_sq, u_rl2, 1, scale=2.0 ** 40)
            for q in range(B):
                act.wait_ge(fT_ps, q + 1)
                ac(fT[:, q * S:q * S + S], bank[q % 2][0:D, :], ACT.Copy).then_inc(fT_sb, 1)

            def all_tokens(q, free):
                n = q * TILES
                tiles = PARTS[q][1] - PARTS[q][0]
                w = P * tiles

                def expo(j):
                    act.wait_ge(score_ps, n + j + 1)
                    act.wait_ge(mixed, max(n + j - 1, 0))
                    ac(esc[:, j % 2, 0:w], bank[4 + j % 2][:, 0:w], ACT.Exp).then_inc(score_exp, 1)

                expo(0)
                yield
                for j in range(TILES):
                    if j + 1 < TILES:
                        expo(j + 1)
                    if j % 2 == 1:
                        yield
                act.wait_ge(mixed, n + TILES)
                act.wait_ge(mixT_ps, q)
                ac(uT[:, 0:w], bank[7][0:D + 1, 0:w], ACT.Copy).then_inc(mix_sb, 1)
                yield
                rstd(few(NM, tiles), m_sq, m_rl2, q, scale=2.0 ** 40)
                yield
                yield

            def turn_kT(b, j, c):
                p = (b * TPB + j) * 4 + c
                act.wait_ge(kT_ps, p + 1)
                ac(kT[:, b % 2, c, P * j:P * j + P], bank[3][:, 0:P], ACT.Copy).then_inc(kT_sb, 1)

            def weigh(b, j, hd):
                pass

            def add_up(b, j, hd):
                m = (b * TPB + j) * HEADS + hd
                ps = bank[3 * (hd % 2)]
                act.wait_ge(summed, SLOTS + m + 1)
                ac(k_now[:, D * hd:D * hd + D], ps[:, 0:D], ACT.Copy)
                ac(val[:, b % 2, j, hd, :], ps[:, D:2 * D], ACT.Copy).then_inc(kv_sb, 1)

            def route_norm(b, lo=0, hi=TPB):
                n = norms(b, hi)
                rstd(few(NR, hi - lo), r_var, r_rstd, n)
                yield from idle(2)
                act.wait_ge(r_xT_ps, n + 1)
                ac(xT[:, bass.ds((b % XRING) * S + P * lo, P * (hi - lo))], bank[1][0:D, 0:P * (hi - lo)], ACT.Copy).then_inc(r_xT, 1)
                yield

            def route(t):
                act.wait_ge(q_ps, t + 1)
                ac(qpkT[:, :, :].rearrange("p c t -> p (c t)"), bank[1][:, :], ACT.Copy).then_inc(q_sb, 1)
                yield
                act.wait_ge(sim_ps, t + 1)
                act.wait_ge(picked, t)
                for i in range(2):
                    last = ac(sim[:, 8 * i:8 * i + 8, :].rearrange("p r k -> p (r k)"), bank[1 + i][:, :], ACT.Copy)
                last.then_inc(sim_sb, 1)
                yield from idle(5)
                act.wait_ge(shifted, t + 1)
                ac(shift[:], shift[:], ACT.Exp).then_inc(exped, 1)
                yield from idle(6)

            def attend(b, i, free):
                t = b * TPB + i
                g = t * HEADS

                def expo(u):
                    w = P * (i + 1)
                    act.wait_ge(a_max, g + u + 1)
                    ac(prob[:, u % 2, 0:w], bank[4 + u % 2][:, 0:w], ACT.Exp, bias=negmax[:, u % 2:u % 2 + 1],
                       accum_out=psum_row[:, u % 4:u % 4 + 1]).then_inc(a_exp, 1)

                act.wait_ge(aq_ps, t + 1)
                for half in range(2):
                    r = slice(D * half, D * half + D)
                    last = ac(qz[r, half::2, :], bank[6][r, :].rearrange("p (c t) -> p c t", t=P), ACT.Copy,
                              scale=D ** -0.5)
                last.then_inc(aq_sb, 1)
                yield
                expo(0)
                yield
                for u in range(HEADS):
                    if u + 1 < HEADS:
                        expo(u + 1)
                    act.wait_ge(a_T, g + u + 1)
                    act.wait_ge(a_o, count(g + u - 1))
                    ac(probT[:, u % 2, 0:i + 1, :], bank[6][:, 0:P * (i + 1)].rearrange("p (c t) -> p c t", t=P),
                       ACT.Copy).then_inc(a_Tsb, 1)
                    yield
                yield
                act.wait_ge(ao_T, t + 1)
                ac(oT[:], bank[6][:, :].rearrange("p (c t) -> p c t", t=P), ACT.Copy).then_inc(ao_sb, 1)
                yield
                yield

            def gates(b):
                rstd(NM, m_var, m_rstd, b)
                yield from idle(2)
                act.wait_ge(m_xT_ps, b + 1)
                ac(xt4, bank[4][0:D, :], ACT.Copy).then_inc(m_xT, 1)
                yield
                for c in range(4):
                    act.wait_ge(xz_ps, 4 * b + c + 1)
                    ac(xz[:, c, :], bank[4 + (c + 1) % 4][:, :], ACT.Copy, accum_out=xsum[:, c:c + 1]).then_inc(xz_sb, 1)
                yield from idle(2)
                act.wait_ge(gsh_in, b + 1)
                for c in range(4):
                    last = ac(gate[:, c, :], xz[:, c, :], ACT.Exp, bias=ngsh[:, c:c + 1], scale=-1.0)
                last.then_inc(sig_e, 1)
                yield from idle(3)

            def direction(b, d, tiles):
                m = b * 2 + d
                n0 = m * NST

                def decay(n):
                    if n >= 2:
                        act.wait_ge(scanned, n0 + n - 1)
                    ac(dA[:, n % 2, :], dt[:], ACT.Exp, scale=negA[:, d, n:n + 1]).then_inc(dA_in, 1)

                act.wait_ge(xd_ps, m + 1)
                ac(bc3[:], bank[6][:, :], ACT.Copy)
                ac(dt_low, bank[6][0:RANK, :], ACT.Copy).then_inc(xd_sb, 1)
                yield
                act.wait_ge(dt_ps, m + 1)
                ac(sp_relu, bank[7][:, :], ACT.Relu, bias=bdt[:, d:d + 1])
                ac(sp_w, bank[7][:, :], ACT.Abs, bias=bdt[:, d:d + 1])
                act.drain()
                ac(sp_u, sp_w, ACT.Exp, scale=-1.0).then_inc(sp_e, 1)
                yield from idle(2)
                act.wait_ge(dt_in, m + 1)
                decay(0)
                yield
                for n in range(NST):
                    if n + 1 < NST:
                        decay(n + 1)
                    yield
                yield from idle(2)

            def mix_out(b):
                yield from idle(OUT_STEPS)

            def experts(b):
                rstd(NM, e_var, e_rstd, b)
                yield from idle(2)
                act.wait_ge(e_xT_ps, b + 1)
                ac(xt4, bank[4][0:D, :], ACT.Copy).then_inc(e_xT, 1)
                yield
                act.wait_ge(m_done, b + 1)
                for e in range(EXP):
                    act.wait_ge(hid_ps, EXP * b + e + 1)
                    ac(hid[:, e, :], bank[6 + e % 2][:, :], ACT.Relu, bias=eb1[:, e:e + 1]).then_inc(hid_sb, 1)
                    if e == 3:
                        act.wait_ge(top_d, b + 1)
                        ac(tw[:, 1, :], tw[:, 0, :], ACT.Exp).then_inc(top_e, 1)
                    if e % 2 == 1:
                        yield
                yield from idle(5)

            schedule(act, all_tokens, lambda t, parity: None, (weigh, add_up, turn_kT), route_norm, route, attend, gates, direction, mix_out, experts)

        @block.vector
        def _(dve):
            tt, ts, stt = dve.tensor_tensor, dve.tensor_scalar, dve.scalar_tensor_tensor

            def seq(*ops):
                for i, op in enumerate(ops):
                    last = op()
                    if i + 1 < len(ops):
                        dve.drain()
                return last

            def newton(N, v):
                return (lambda: tt(N["t"][:], N["y0"][:], N["y0"][:], ALU.mult),
                        lambda: tt(N["t"][:], N["t"][:], v, ALU.mult),
                        lambda: ts(N["t"][:], N["t"][:], -0.5, 1.5, ALU.mult, ALU.add),
                        lambda: tt(N["r"][:], N["t"][:], N["y0"][:], ALU.mult))

            def centre(N, src, done_v):
                shape = [P, N["s"].shape[1], D]
                seq(lambda: dve.tensor_reduce(N["s"][:], src, AX.X, ALU.add),
                    lambda: stt(out=N["xc"][:], in0=bc(N["s"][:], shape, 2), scalar=-1.0 / D, in1=src,
                                op0=ALU.mult, op1=ALU.add),
                    lambda: tt(N["sq"][:], N["xc"][:], N["xc"][:], ALU.mult),
                    lambda: dve.tensor_reduce(N["s"][:], N["sq"][:], AX.X, ALU.add),
                    lambda: ts(N["v"][:], N["s"][:], 1.0 / D, EPS, ALU.mult, ALU.add).then_inc(done_v, 1))

            def scaled(N, done_r, n):
                dve.wait_ge(done_r, n + 1)
                shape = [P, N["s"].shape[1], D]
                return seq(*newton(N, N["v"][:]),
                           lambda: tt(N["sq"][:], N["xc"][:], bc(N["r"][:], shape, 2), ALU.mult))

            dve.memset(fsum[:], 0.0).then_inc(summed, SLOTS)
            dve.wait_ge(consts, 1)
            dve.wait_ge(ids_in, 16)
            dve.wait_ge(w_feat_in, 16)
            col = [w_feat[:, i:i + 1] for i in range(5)]
            seq(lambda: dve.tensor_copy(ang, idsb),
                lambda: ts(ang, ang, TWO_PI, col[0], ALU.mult, ALU.mult),
                lambda: ts(ang, ang, col[1], col[4], ALU.mult, ALU.add),
                lambda: ts(turn, ang, col[2], 1.0 / TWO_PI, ALU.add, ALU.mult),
                lambda: ts(turn, turn, ROUND, -ROUND, ALU.add, ALU.add),
                lambda: stt(out=ang, in0=turn, scalar=-PI_A, in1=ang, op0=ALU.mult, op1=ALU.add),
                lambda: stt(out=ang, in0=turn, scalar=-PI_B, in1=ang, op0=ALU.mult, op1=ALU.add),
                lambda: stt(out=ang, in0=turn, scalar=-PI_C, in1=ang, op0=ALU.mult, op1=ALU.add),
                lambda: ts(ang, ang, col[2], PI_MAX, ALU.add, ALU.min),
                lambda: ts(ang, ang, -PI_MAX, None, ALU.max).then_inc(angle_done, 1))
            dve.wait_ge(feat_done, 1)
            ts(feat, feat, col[3], None, ALU.mult).then_inc(scaled_feat, 1)
            row = [bc(trow[:, i, :], [P, TPB, D], 1) for i in range(4)]
            row16 = [bc(trow[:, i, :], half, 1) for i in range(4)]
            dve.wait_ge(loaded, 16 * LOADS)

            def embed(n):
                dve.wait_ge(h2_ps, n + 1)
                ps = bank[2 + n % 2]
                to = slice(TPB * (n % GROUPS), TPB * (n % GROUPS) + TPB)
                tt(NE[n // GROUPS]["sq"][:, to, :], ps[:, 0:256].rearrange("p (j d) -> p j d", d=D), row[0], ALU.add)
                tt(h[:, TPB * n:TPB * n + TPB, :], ps[:, 256:512].rearrange("p (j d) -> p j d", d=D), row[3],
                   ALU.add).then_inc(h2_read, 1)
                dve.drain()

            def unit_vectors(i):
                N = NE[i]
                here = slice(TILES // 2 * i, TILES // 2 * (i + 1))
                centre(N, N["sq"], t_var)
                yield
                scaled(N, t_rstd, i)
                dve.drain()
                seq(lambda: tt(N["sq"], N["sq"], row16[1], ALU.mult),
                    lambda: tt(N["sq"], N["sq"], row16[2], ALU.add),
                    lambda: stt(out=h[:, here, :], in0=h[:, here, :], scalar=0.1, in1=N["sq"], op0=ALU.mult,
                                op1=ALU.add))
                dve.drain()
                yield
                centre(N, h[:, here, :], u_var)
                yield
                dve.wait_ge(u_rstd, i + 1)
                seq(*newton(N, N["v"]),
                    lambda: tt(N["r1"], N["r"], N["r"], ALU.mult),
                    lambda: tt(N["v"], N["r1"], N["s"], ALU.mult),
                    lambda: ts(N["v"], N["v"], 1e-24, None, ALU.max).then_inc(u_sq, 1),
                    lambda: dve.tensor_copy(N["r1"], N["r"]))
                yield
                dve.wait_ge(u_rl2, i + 1)
                seq(lambda: ts(N["y0"], N["y0"], 2.0 ** 20, None, ALU.mult),
                    *newton(N, N["v"]),
                    lambda: tt(N["r"], N["r"], N["r1"], ALU.mult))
                dve.drain()
                yield

            for n in range(GROUPS):
                embed(n)
            first, second = unit_vectors(0), unit_vectors(1)
            next(first)
            for n in range(GROUPS, 2 * GROUPS):
                embed(n)
                next(first)
            for _ in second:
                pass
            dve.memset(f1[:, :, D:D + 1], 1.0)
            for i in range(2):
                tt(f1[:, TILES // 2 * i:TILES // 2 * (i + 1), 0:D], NE[i]["xc"], bc(NE[i]["r"], half, 2),
                   ALU.mult).then_inc(f_done, 1)
            dve.drain()
            tt(spread3[:], idb[:, 32:64], idb[:, 64:96], ALU.add)
            dve.drain()
            tt(spread3[:], spread3[:], idb[:, 96:128], ALU.add)
            dve.drain()

            def all_tokens(q, free):
                lo, hi = PARTS[q]
                here = slice(lo, hi)
                N = few(NM, hi - lo)
                wide = [P, hi - lo, D]
                yield from idle(PART_STEPS - 2)
                dve.wait_ge(mixT_ps, q + 1)
                mixT = bank[6][:, 0:(hi - lo) * (D + 1)].rearrange("p (j d) -> p j d", d=D + 1)
                seq(lambda: dve.reciprocal(tw[:, 0, 0:hi - lo].unsqueeze(2), mixT[:, :, D:D + 1]),
                    lambda: ts(tw[:, 0, 0:hi - lo], tw[:, 0, 0:hi - lo], 1.0 - 0.8, None, ALU.mult),
                    lambda: tt(N["xc"][:], mixT[:, :, 0:D], bc(tw[:, 0, 0:hi - lo], wide, 2),
                               ALU.mult).then_inc(mixT_read, 1),
                    lambda: stt(out=N["xc"][:], in0=f1[:, here, 0:D], scalar=0.8, in1=N["xc"][:],
                                op0=ALU.mult, op1=ALU.add),
                    lambda: tt(N["sq"][:], N["xc"][:], N["xc"][:], ALU.mult),
                    lambda: dve.tensor_reduce(N["s"][:], N["sq"][:], AX.X, ALU.add),
                    lambda: ts(N["v"][:], N["s"][:], 1e-24, None, ALU.max).then_inc(m_sq, 1))
                yield
                dve.wait_ge(m_rl2, q + 1)
                seq(lambda: ts(N["y0"][:], N["y0"][:], 2.0 ** 20, None, ALU.mult),
                    *newton(N, N["v"][:]),
                    lambda: tt(N["xc"][:], N["xc"][:], bc(N["r"][:], wide, 2), ALU.mult),
                    lambda: tt(h[:, here, :], h[:, here, :], N["xc"][:], ALU.add))
                dve.drain()
                yield

            def turn_kT(b, j, c):
                pass

            def add_up(b, j, hd):
                pass

            def hand_over(t, parity):
                dve.wait_ge(routed, t + 1)
                settle(dve)
                dve.tensor_copy(ids_now[:, parity, :], ids_ring[:, t % RING, :]).then_inc(ids_ready, 1)

            def weigh(b, j, hd):
                t = b * TPB + j
                slot = hd % SLOTS
                if hd == (5 if t_is(b, j, 0) else 3) and not t_is(b, j, TILES - 1):
                    hand_over(t + 1, (j + 1) % 2)
                dve.wait_ge(landed[slot], 16 * TOPK * (t * (HEADS // SLOTS) + hd // SLOTS + 1))
                last = tt(rows[:, slot, :, :], rows[:, slot, :, :],
                          bc(w_ring[:, t % RING, TOPK * hd:TOPK * hd + TOPK], [P, TOPK, 2 * D], 2), ALU.mult)
                n = TOPK
                while folds(b) and n > FOLD:
                    n //= 2
                    dve.drain()
                    last = tt(rows[:, slot, 0:n, :], rows[:, slot, 0:n, :], rows[:, slot, n:2 * n, :], ALU.add)
                last.then_inc(weighted, 1)

            def route_norm(b, lo=0, hi=TPB):
                n = norms(b, hi)
                N = few(NR, hi - lo)
                dve.wait_ge(r_xT_ps, n)
                centre(N, h[:, bass.ds(b * TPB + lo, hi - lo), :], r_var)
                yield
                scaled(N, r_rstd, n).then_inc(r_x, 1)
                yield
                yield

            def route(t):
                ring = t % RING
                yield from idle(2)
                dve.wait_ge(sim_sb, t + 1)
                settle(dve)
                rr = range(ROWS)
                for r in rr:
                    dve.max(best[:, r, 0:8], sim[:, r, :])
                dve.drain()
                yield
                for r in rr:
                    dve.match_replace(sim2[:, r, :], best[:, r, 0:8], sim[:, r, :], LOW)
                    last = dve.max_index(besti[:, r, 0:8], best[:, r, 0:8], sim[:, r, :])
                last.then_inc(picked, 1)
                dve.drain()
                yield
                for r in rr:
                    dve.max(best[:, r, 8:16], sim2[:, r, :])
                dve.drain()
                for r in rr:
                    dve.max_index(besti[:, r, 8:16], best[:, r, 8:16], sim2[:, r, :])
                dve.drain()
                tt(bestf[:, 0:HEADS, :], besti[:, 0:HEADS, :], head_base[:], ALU.add)
                ts(bestf[:, HEADS:ROWS, :], besti[:, HEADS:ROWS, :], float(NKEY), None, ALU.mult)
                dve.drain()
                yield
                for src, dst in ((best, cval), (bestf, cid)):
                    at = 0
                    for a in range(WIDE):
                        n = CAND[a]
                        tt(dst[:, :, at:at + n], src[:, 0:HEADS, a:a + 1].broadcast_to([P, HEADS, n]),
                           src[:, HEADS:ROWS, 0:n], ALU.add)
                        at += n
                    n = TOPK - WIDE
                    tt(dst[:, :, at:at + n], src[:, 0:HEADS, WIDE:TOPK],
                       src[:, HEADS:ROWS, 0:1].broadcast_to([P, HEADS, n]), ALU.add)
                dve.drain()
                hh = range(HEADS)
                for r in hh:
                    dve.max(fval[:, r, 0:8], cval[:, r, :])
                dve.drain()
                yield
                for r in hh:
                    dve.match_replace(cval2[:, r, :], fval[:, r, 0:8], cval[:, r, :], LOW)
                    dve.max_index(fpos[:, r, 0:8], fval[:, r, 0:8], cval[:, r, :])
                dve.drain()
                for r in hh:
                    dve.max(fval[:, r, 8:16], cval2[:, r, :])
                dve.drain()
                for r in hh:
                    dve.max_index(fpos[:, r, 8:16], fval[:, r, 8:16], cval2[:, r, :])
                tt(shift[:], fval[:], fval[:, :, 0:1].broadcast_to([P, HEADS, TOPK]),
                   ALU.subtract).then_inc(shifted, 1)
                dve.drain()
                dve.tensor_copy(fposf[:], fpos[:])
                dve.drain()
                yield
                for q in range(HEADS // LOOKUP):
                    hs = slice(LOOKUP * q, LOOKUP * q + LOOKUP)
                    full = [P, LOOKUP, TOPK, NCAND]
                    lk = look[:, :].rearrange("p (a k c) -> p a k c", a=LOOKUP, k=TOPK)
                    lk2 = look[:, :].rearrange("p (r c) -> p r c", c=NCAND)
                    two = [P, LOOKUP * TOPK, NCAND]
                    tt(lk2, bc(fposf[:, hs, :].rearrange("p a k -> p (a k)"), two, 2), bc(cand_no[:], two, 1),
                       ALU.is_equal)
                    dve.drain()
                    tt(lk, lk, bc(cid[:, hs, :], full, 2), ALU.mult)
                    dve.drain()
                    dve.tensor_reduce(fposf[:, hs, :].rearrange("p a k -> p (a k)"), lk2, AX.X, ALU.add)
                    dve.drain()
                    yield
                dve.tensor_copy(ids_ring[:, ring, :], fposf[:, :, :].rearrange("p a k -> p (a k)")).then_inc(routed, 1)
                dve.wait_ge(exped, t + 1)
                seq(lambda: dve.tensor_reduce(fsum[:], shift[:], AX.X, ALU.add),
                    lambda: dve.reciprocal(fsum[:], fsum[:]),
                    lambda: tt(w_ring[:, ring, :].rearrange("p (a k) -> p a k", k=TOPK), shift[:],
                               bc(fsum[:], [P, HEADS, TOPK], 2), ALU.mult))
                dve.drain()
                yield

            def attend(b, i, free):
                t = b * TPB + i
                g = t * HEADS

                def row_max(u):
                    dve.wait_ge(a_s, g + u + 1)
                    dve.tensor_reduce(negmax[:, u % 2:u % 2 + 1], bank[4 + u % 2][:, 0:P * (i + 1)], AX.X, ALU.max,
                                      negate=True).then_inc(a_max, 1)

                def normalise(u):
                    dve.wait_ge(a_o, g + u + 1)
                    dve.reciprocal(rrow[:], psum_row[:, u % 4:u % 4 + 1])
                    dve.drain()
                    ts(o_now[:, D * u:D * u + D], bank[7][:, 0:D], rrow[:, 0:1], None, ALU.mult).then_inc(a_norm, 1)
                    dve.drain()

                yield
                row_max(0)
                yield
                for u in range(HEADS):
                    if u >= 2:
                        normalise(u - 2)
                    if u + 1 < HEADS:
                        row_max(u + 1)
                    yield
                normalise(HEADS - 2)
                normalise(HEADS - 1)
                yield
                yield
                dve.wait_ge(ao_ps, t + 1)
                hi = h[:, t, :]
                tt(hi, hi, bank[7][:, 0:D], ALU.add).then_inc(ao_h, 1)
                dve.drain()
                yield

            def gates(b):
                tile4 = bass.ds(b * TPB, TPB)
                centre(NM, h[:, tile4, :], m_var)
                yield
                scaled(NM, m_rstd, b).then_inc(m_x, 1)
                yield from idle(3)
                dve.wait_ge(xz_sb, 4 * b + 4)
                ts(xmean[:], xsum[:], 1.0 / S, None, ALU.mult).then_inc(mean_in, 1)
                yield
                dve.wait_ge(gsh_ps, b + 1)
                seq(lambda: tt(gsh[:], bank[5][:, 0:4], bg_m[:], ALU.add),
                    lambda: ts(ngsh[:], gsh[:], -1.0, None, ALU.mult).then_inc(gsh_in, 1))
                yield
                dve.wait_ge(sig_e, b + 1)
                g2 = gate[:, :, :].rearrange("p c s -> p (c s)")
                seq(lambda: ts(g2, g2, 1.0, None, ALU.add),
                    lambda: dve.reciprocal(g2, g2))
                dve.drain()
                yield
                for c in (0, 2, 1, 3):
                    last = stt(out=xz[:, c, :], in0=xz[:, c, :], scalar=gsh[:, c:c + 1], in1=gate[:, c, :],
                               op0=ALU.add, op1=ALU.mult)
                last.then_inc(act_in, 1)
                dve.drain()
                yield

            def direction(b, d, tiles):
                m = b * 2 + d
                n0 = m * NST
                xa, zs = xz[:, 2 * d, :], xz[:, 2 * d + 1, :]
                yield
                dve.wait_ge(xd_sb, m + 1)
                seq(lambda: tt(bc_rest[D:P, :], bank[6][D:P, :], bc3[D:P, :], ALU.subtract),
                    lambda: dve.tensor_copy(bc3[D:P, :], bc_rest[D:P, :]),
                    lambda: tt(bc3[96:P, :], bc_rest[96:P, :], bc3[96:P, :], ALU.subtract).then_inc(bc_in, 1))
                dve.drain()
                yield
                dve.wait_ge(sp_e, m + 1)
                seq(lambda: ts(sp_w, sp_u, 2.0, None, ALU.add),
                    lambda: dve.reciprocal(sp_w, sp_w),
                    lambda: tt(sp_u, sp_u, sp_w, ALU.mult),
                    lambda: tt(sp_w, sp_u, sp_u, ALU.mult),
                    lambda: ts(sp_l, sp_w, ATANH[-1], None, ALU.mult))
                dve.drain()
                yield
                seq(*(lambda c=c: stt(out=sp_l, in0=sp_l, scalar=c, in1=sp_w, op0=ALU.add, op1=ALU.mult)
                      for c in ATANH[-2:0:-1]),
                    lambda: stt(out=sp_l, in0=sp_l, scalar=ATANH[0], in1=sp_u, op0=ALU.add, op1=ALU.mult),
                    lambda: tt(dt[:], sp_l, sp_relu, ALU.add).then_inc(dt_in, 1),
                    lambda: tt(dtu[:], dt[:], xa, ALU.mult))
                dve.drain()
                yield
                way = slice(None) if d == 0 else slice(None, None, -1)
                for n in range(NST):
                    dve.wait_ge(B_ps, n0 + n + 1)
                    tt(dBu, dtu[:], bank[4 + 2 * (n % 2)][:, :], ALU.mult).then_inc(dBu_in, 1)
                    dve.drain()
                    dve.wait_ge(dA_in, n0 + n + 1)
                    dve.tensor_tensor_scan(hst[:, way], dA[:, n % 2, way], dBu[:, way], 0.0, ALU.mult,
                                           ALU.add).then_inc(scanned, 1)
                    dve.drain()
                    dve.wait_ge(C_ps, n0 + n + 1)
                    if n >= 2:
                        dve.wait_ge(y_ps, n0 + n - 1)
                    tt(hC[:, n % 2, :], hst, bank[5][:, :], ALU.mult).then_inc(hC_in, 1)
                    yield
                yield
                dve.wait_ge(y_ps, n0 + NST)
                seq(lambda: stt(out=xa, in0=xa, scalar=Dskip[:, d:d + 1], in1=bank[7][:, :], op0=ALU.mult,
                                op1=ALU.add),
                    lambda: tt(gate[:, 2 * d, :], xa, zs, ALU.mult).then_inc(y_in, 1))
                dve.drain()
                yield

            def mix_out(b):
                tile4 = bass.ds(b * TPB, TPB)
                yield
                dve.wait_ge(m_out_ps, b + 1)
                tt(h[:, tile4, :], h[:, tile4, :], bank[6][:, 0:TPB * D].rearrange("p (j d) -> p j d", d=D),
                   ALU.add).then_inc(m_done, 1)
                dve.drain()
                yield

            def experts(b):
                tile4 = bass.ds(b * TPB, TPB)
                centre(NM, h[:, tile4, :], e_var)
                yield
                scaled(NM, e_rstd, b).then_inc(e_x, 1)
                yield from idle(2)
                dve.wait_ge(lg_ps, b + 1)
                four = [P, TPB, EXP]
                tt(lg[:], bank[5][:, 0:TPB * EXP].rearrange("p (j e) -> p j e", e=EXP), bc(ebias[:, 0, :], four, 1),
                   ALU.add).then_inc(lg_read, 1)
                dve.drain()
                tt(lg[:], lg[:], bc(ebias[:, 1, :], four, 1), ALU.add)
                dve.drain()
                yield
                for j in range(TPB):
                    dve.max(lmax[:, j, :], lg[:, j, :])
                dve.drain()
                for j in range(TPB):
                    dve.max_index(lidx[:, j, :], lmax[:, j, :], lg[:, j, :])
                tt(tw[:, 0, :].unsqueeze(2), lmax[:, :, 1:2], lmax[:, :, 0:1], ALU.subtract).then_inc(top_d, 1)
                dve.drain()
                dve.tensor_copy(lidf[:], lidx[:])
                yield
                dve.wait_ge(top_e, b + 1)
                seq(lambda: ts(tw[:, 2, :], tw[:, 1, :], 1.0, None, ALU.add),
                    lambda: dve.reciprocal(tw[:, 2, :], tw[:, 2, :]),
                    lambda: tt(tw[:, 3, :], tw[:, 1, :], tw[:, 2, :], ALU.mult))
                dve.drain()
                for i in range(2):
                    tt(comb[:, i, :, :], bc(exp_no[:], four, 1), lidf[:, :, i:i + 1].broadcast_to(four), ALU.is_equal)
                dve.drain()
                yield
                for i in range(2):
                    tt(comb[:, i, :, :], comb[:, i, :, :], bc(tw[:, 2 + i, :], four, 2), ALU.mult)
                dve.drain()
                tt(comb[:, 0, :, :], comb[:, 0, :, :], comb[:, 1, :, :], ALU.add)
                dve.drain()
                yield
                yield
                for j in range(TPB):
                    dve.wait_ge(y2_ps, TPB * b + j + 1)
                    mixv = gate[:, j, :].rearrange("p (e d) -> p e d", d=D)
                    tt(mixv, bank[4 + j % 2][:, :].rearrange("p (e d) -> p e d", d=D),
                       bc(comb[:, 0, j, :], [P, EXP, D], 2), ALU.mult).then_inc(y2_read, 1)
                    dve.drain()
                    dve.tensor_reduce(ymix[:, j, :], gate[:, j, :].rearrange("p (e d) -> p d e", d=D), AX.X, ALU.add)
                    if j + 1 < TPB:
                        yield
                dve.drain()
                dve.wait_ge(stored, 16 * b + 16)
                tt(hout[:], h[:, tile4, :], ymix[:], ALU.add).then_inc(e_done, 1)
                dve.drain()
                yield

            schedule(dve, all_tokens, hand_over, (weigh, add_up, turn_kT), route_norm, route, attend, gates, direction, mix_out, experts)


def kernel(**inputs):
    import numpy as np
    import concourse.bacc as bacc
    from concourse.bass_utils import run_bass_kernel_spmd

    a = {k: np.asarray(v) for k, v in inputs.items()}
    f = np.float32
    arrays = {n: a[n] for n in (
        "L0_tok_b1", "L0_tok_W2", "L0_tok_b2", "L0_tok_gamma", "L0_tok_beta", "L0_tok_bres", "L0_ffn_Wq_pk", "L0_ffn_Wq", "L0_ffn_Wo",
        "L1_attn_b_dt_f", "L1_attn_b_dt_b", "L1_attn_A_log_f", "L1_attn_A_log_b", "L1_attn_D_f", "L1_attn_D_b",
        "L1_ffn_Wg", "L1_ffn_bg", "L1_ffn_bias", "L1_ffn_W1", "L1_ffn_W2", "L1_ffn_b2")}
    w = np.zeros((GROUPS, 32, 5 + 128 + D), f)
    w[:, 0:FD, 0:3] = [[1.0 / p, k, c] for p in (7.0, 24.0, 12.0, 1.0) for k in range(1, HARM + 1)
                       for c in (0.0, TWO_PI / 4)]
    w[:, 0:FD, 3] = np.repeat(a["L0_tok_hw"].reshape(-1), 2)
    w[:, 0:FD, 4] = np.repeat(a["L0_tok_ph"].reshape(-1), 2)
    w[:, 0:FD, 5:5 + 128] = a["L0_tok_W1"]
    w[:, 0:FD, 5 + 128:] = a["L0_tok_Wres"]
    arrays["feature_weights"] = w.reshape(P, 5 + 128 + D)
    ids = np.zeros((GROUPS, 32, 2, S), np.int32)
    for k, n in enumerate(("x", "itok_BS_0_23", "itok_BS_0_11", "itok_BS_0_30")):
        ids[:, 2 * HARM * k:2 * HARM * (k + 1)] = a[n].reshape(2, GROUPS, S).transpose(1, 0, 2)[:, None]
    arrays["ids_by_feature"] = ids.reshape(P, GTOK)
    arrays["keysT"] = a["L0_ffn_pk_keys"].transpose(0, 2, 3, 1).reshape(ROWS, KDIM, NKEY)
    arrays["kv_table"] = np.concatenate([a["L0_ffn_keys_table"], a["L0_ffn_values_table"]], axis=1)
    arrays["W_inT"] = a["L1_attn_W_in"].T
    arrays["W_gT"] = a["L1_attn_W_g"].T
    arrays["b_gT"] = a["L1_attn_b_g"].reshape(4, DI).T
    for s in "fb":
        arrays["W_xpT_" + s] = a["L1_attn_W_xp_" + s].T
        arrays["W_dtT_" + s] = a["L1_attn_W_dt_" + s].T
    arrays["W_outT"] = a["L1_attn_W_out"].T
    arrays["eb1T"] = a["L1_ffn_b1"].T
    arrays = {k: np.ascontiguousarray(v) for k, v in arrays.items()}

    nc = bacc.Bacc("TRN2", target_bir_lowering=False, num_devices=1)
    A = {k: nc.dram_tensor("in_" + k, v.shape, mybir.dt.from_np(v.dtype), kind="ExternalInput").ap()
         for k, v in arrays.items()}
    out = nc.dram_tensor("out", (B, S, D), F32, kind="ExternalOutput").ap()
    program(nc, A, out)
    r = run_bass_kernel_spmd(nc, [{"in_" + k: v for k, v in arrays.items()}], core_ids=[0])
    return r.results[0]["out"]
```
